# Optimizing a Trainium2 kernel written in Bass

```python
import numpy as np
import jax
import jax.numpy as jnp

def _softmax(x, axis=-1):
    return jax.nn.softmax(x, axis=axis)

def _gelu(x):
    return jax.nn.gelu(x, approximate=True)

def _silu(x):
    return jax.nn.silu(x)

def _sigmoid(x):
    return jax.nn.sigmoid(x)

def _layernorm(x, axis=-1, eps=1e-05):
    m = jnp.mean(x, axis=axis, keepdims=True)
    v = jnp.var(x, axis=axis, keepdims=True)
    return (x - m) / jnp.sqrt(v + eps)

def _scatter_add(tgt, idx, src, axis=0):
    return tgt.at[idx].add(src)

def _segment_sum(src, seg, n):
    return jax.ops.segment_sum(src, seg, n)
kernel_name = 'mk_decoder_preln_d1_seqx_r8_b0f0e4'

def setup_inputs(seed: int=0):
    np.random.seed(seed)
    _w = jnp.asarray

    def _rec_inputs():
        import jax
        import jax.numpy as jnp
        _rk = jax.random.key(seed)
        x = 7.22e-05 + 1 * jax.random.normal(jax.random.fold_in(_rk, 1), (64, 64, 128), jnp.float32)
        _lenS = 64 - jax.random.randint(jax.random.fold_in(_rk, 7), (64,), 0, max(1, 64 // 4) + 1, jnp.int32)
        _lenS2 = 64 - jax.random.randint(jax.random.fold_in(_rk, 8), (64,), 0, max(1, 64 // 4) + 1, jnp.int32)
        _ctx_1024P = jax.random.normal(jax.random.fold_in(_rk, 11), (64, 16, 128), jnp.float32)
        _ctx_1024c = jax.random.dirichlet(jax.random.fold_in(_rk, 511), 0.3 * jnp.ones((16,), jnp.float32), (64, 64))
        _ctx_1024t = jnp.einsum('bsk,bkd->bsd', _ctx_1024c, _ctx_1024P)
        _ctx_1024t = _ctx_1024t * jax.lax.rsqrt(jnp.mean(jnp.square(_ctx_1024t)) + 1e-12) * 0.953939
        ctx_1024 = 4.13588e-05 + 0.999923 * (_ctx_1024t + 0.3 * jax.random.normal(jax.random.fold_in(_rk, 611), (64, 64, 128), jnp.float32))
        return (x, ctx_1024)
    x, ctx_1024 = _rec_inputs()

    def _L0_attn_setup():
        import jax, jax.numpy as jnp
        import numpy as np
        import math
        B, S, D, H = (4, 256, 128, 16)
        DK = D // H
        key = jax.random.key(seed)
        ks = jax.random.split(key, 5)
        scale = 1.0 / math.sqrt(D)
        return {'x': jax.random.normal(ks[0], (B, S, D), dtype=jnp.float32), 'Wv': jax.random.normal(ks[1], (D, D), dtype=jnp.float32) * scale, 'bv': jax.random.normal(ks[2], (D,), dtype=jnp.float32) * scale, 'Wo': jax.random.normal(ks[3], (D, D), dtype=jnp.float32) * scale, 'bo': jax.random.normal(ks[4], (D,), dtype=jnp.float32) * scale}
    _L0_attn_all = _L0_attn_setup()
    _L0_attn_in = {k: v for k, v in _L0_attn_all.items() if k in ('Wv', 'bv', 'Wo', 'bo')}
    del _L0_attn_all

    def _L0_xattn_setup():
        import jax, jax.numpy as jnp
        import numpy as np
        NUM_UNITS = 128
        NUM_HEADS = 16
        key = jax.random.key(seed)
        kq, kk, kv = jax.random.split(key, 3)
        B, T, U = (4, 256, NUM_UNITS)
        return {'querys': jax.random.normal(kq, (B, T, U), dtype=jnp.float32), 'keys': jax.random.normal(kk, (B, T, U), dtype=jnp.float32), 'values': jax.random.normal(kv, (B, T, U), dtype=jnp.float32)}
    _L0_xattn_all = _L0_xattn_setup()
    _L0_xattn_in = {k: v for k, v in _L0_xattn_all.items() if k in ()}
    del _L0_xattn_all

    def _L0_ffn_setup():
        import jax, jax.numpy as jnp
        import numpy as np
        B, T, C, I, E = (4, 256, 128, 352, 7)

        def _swiglu(h, w1, w2, w3):
            return jax.nn.silu(h @ w1.T) * (h @ w3.T) @ w2.T
        key = jax.random.key(seed)
        ks = jax.random.split(key, 9)
        sc_c = 1.0 / np.sqrt(C)
        sc_i = 1.0 / np.sqrt(I)
        return {'x': jax.random.normal(ks[0], (B, T, C), jnp.float32), 'router_w': jax.random.normal(ks[1], (E, C), jnp.float32) * sc_c, 'routing_bias': jnp.zeros((E,), jnp.float32), 'sw1': jax.random.normal(ks[2], (I, C), jnp.float32) * sc_c, 'sw2': jax.random.normal(ks[3], (C, I), jnp.float32) * sc_i, 'sw3': jax.random.normal(ks[4], (I, C), jnp.float32) * sc_c, 'ew1': jax.random.normal(ks[5], (E, I, C), jnp.float32) * sc_c, 'ew2': jax.random.normal(ks[6], (E, C, I), jnp.float32) * sc_i, 'ew3': jax.random.normal(ks[7], (E, I, C), jnp.float32) * sc_c}
    _L0_ffn_all = _L0_ffn_setup()
    _L0_ffn_in = {k: v for k, v in _L0_ffn_all.items() if k in ('router_w', 'routing_bias', 'sw1', 'sw2', 'sw3', 'ew1', 'ew2', 'ew3')}
    del _L0_ffn_all
    return {'x': x, 'ctx_1024': ctx_1024, 'L0_attn_Wv': _L0_attn_in['Wv'], 'L0_attn_bv': _L0_attn_in['bv'], 'L0_attn_Wo': _L0_attn_in['Wo'], 'L0_attn_bo': _L0_attn_in['bo'], 'L0_ffn_router_w': _L0_ffn_in['router_w'], 'L0_ffn_routing_bias': _L0_ffn_in['routing_bias'], 'L0_ffn_sw1': _L0_ffn_in['sw1'], 'L0_ffn_sw2': _L0_ffn_in['sw2'], 'L0_ffn_sw3': _L0_ffn_in['sw3'], 'L0_ffn_ew1': _L0_ffn_in['ew1'], 'L0_ffn_ew2': _L0_ffn_in['ew2'], 'L0_ffn_ew3': _L0_ffn_in['ew3']}

def reference(x, ctx_1024, L0_attn_Wv, L0_attn_bv, L0_attn_Wo, L0_attn_bo, L0_ffn_router_w, L0_ffn_routing_bias, L0_ffn_sw1, L0_ffn_sw2, L0_ffn_sw3, L0_ffn_ew1, L0_ffn_ew2, L0_ffn_ew3):
    import jax
    import jax.numpy as jnp

    def _L0_attn_ref(x, Wv, bv, Wo, bo):
        import jax, jax.numpy as jnp
        import numpy as np
        import math
        B, S, D, H = (4, 256, 128, 16)
        DK = D // H
        b, s, d = x.shape
        h, dk = (H, DK)
        p = jnp.einsum('bsd,ed->bse', x, Wv) + bv
        p = p.reshape(b, s, h, dk).transpose(0, 2, 1, 3)
        q = k = v = p
        scores = jnp.einsum('bhqd,bhkd->bhqk', q, k) / math.sqrt(dk)
        attn = jax.nn.softmax(scores, axis=-1)
        out = jnp.einsum('bhqk,bhkd->bhqd', attn, v)
        out = out.reshape(b, s, h * dk)
        return jnp.einsum('bsd,ed->bse', out, Wo) + bo

    def _L0_xattn_ref(querys, keys, values):
        import jax, jax.numpy as jnp
        import numpy as np
        NUM_UNITS = 128
        NUM_HEADS = 16
        B, Tq, U = querys.shape
        Tk = keys.shape[1]
        H = NUM_HEADS
        D = U // H
        q = querys.reshape(B, Tq, H, D).transpose(2, 0, 1, 3)
        k = keys.reshape(B, Tk, H, D).transpose(2, 0, 1, 3)
        v = values.reshape(B, Tk, H, D).transpose(2, 0, 1, 3)
        scores = jnp.einsum('hbqd,hbkd->hbqk', q, k) / jnp.sqrt(jnp.float32(D))
        probs = jax.nn.softmax(scores, axis=3)
        out = jnp.einsum('hbqk,hbkd->hbqd', probs, v)
        return out.transpose(1, 2, 0, 3).reshape(B, Tq, H * D)

    def _L0_ffn_ref(x, router_w, routing_bias, sw1, sw2, sw3, ew1, ew2, ew3):
        import jax, jax.numpy as jnp
        import numpy as np
        B, T, C, I, E = (4, 256, 128, 352, 7)

        def _swiglu(h, w1, w2, w3):
            return jax.nn.silu(h @ w1.T) * (h @ w3.T) @ w2.T
        b, t, c = x.shape
        shared_out = _swiglu(x, sw1, sw2, sw3)
        logits = jnp.clip(x @ router_w.T + routing_bias, -50.0, 50.0)
        probs = jax.nn.sigmoid(logits)
        num_switched = 1
        topk_probs, topk_idx = jax.lax.top_k(probs, num_switched)
        topk_probs = jnp.clip(topk_probs, 1e-08, 1.0 - 1e-08)
        xf = x.reshape(-1, c)
        sel = topk_idx.reshape(-1)
        p = topk_probs.reshape(-1)
        switched = jnp.zeros_like(xf)
        n_experts = ew1.shape[0]
        for e in range(n_experts):
            y = _swiglu(xf, ew1[e], ew2[e], ew3[e])
            w = jnp.where(sel == e, p, 0.0)
            switched = switched + w[:, None] * y
        switched = switched.reshape(b, t, c)
        total_weight = 0.5 + topk_probs.sum(axis=-1)
        total_weight = jnp.clip(total_weight[..., None] + 1e-08, 0.5, 2.0)
        return 0.5 / total_weight * shared_out + switched / total_weight
    x = x + _L0_attn_ref(_layernorm(x, axis=-1), L0_attn_Wv, L0_attn_bv, L0_attn_Wo, L0_attn_bo)
    x = x + _L0_xattn_ref(_layernorm(x, axis=-1), ctx_1024, ctx_1024)
    x = x + _L0_ffn_ref(_layernorm(x, axis=-1), L0_ffn_router_w, L0_ffn_routing_bias, L0_ffn_sw1, L0_ffn_sw2, L0_ffn_sw3, L0_ffn_ew1, L0_ffn_ew2, L0_ffn_ew3)
    return x

_drawn_inputs = setup_inputs


def setup_inputs(seed=0):
    import zlib

    import numpy as np

    out = dict(_drawn_inputs(seed))
    spreads = {'L0_ffn_routing_bias': (0.0, 0.1)}
    factors = {}
    for name, (base, spread) in spreads.items():
        noise = np.random.default_rng([zlib.crc32(name.encode()), seed]).standard_normal(out[name].shape)
        drawn = base * np.exp(spread * noise) if base else spread * noise
        out[name] = jnp.asarray(drawn.astype(out[name].dtype))
    for name, factor in factors.items():
        out[name] = (out[name] * factor).astype(out[name].dtype)
    return out
```

```python
from contextlib import ExitStack

import concourse.bass as bass
from concourse import mybir

P = 128
D = 128
S = 64
B = 64
H = 16
DK = D // H
NB = P // S
U = B // NB
G = 2
HG = H // G
HP = H // 2
E = 7
NE = E + 1
I = 352
NTOK = B * S
CH = 3
LAST = I - (CH - 1) * P
SLOTS = (NTOK + E * (P - 1)) // P
ROW = 2 * D + 2
WT, TOK = 2 * D, 2 * D + 1
VW = 2 * NB * (DK + 1)
VALL = 384
NOWHERE = 1.0e6
EPS = 1e-5
KNEE = 8.0
Q_KNEE = 1.0 + 2.718281828459045 ** -KNEE
F32 = mybir.dt.float32
I32 = mybir.dt.int32
ALU = mybir.AluOpType
ACT = mybir.ActivationFunctionType
AX = mybir.AxisListType


def build(nc, x, ctxk, ctxv, wv, bv, wo, bo, rw, rb, wup, wdn, ident, hmask, tri, small, tokens, out):
    ctx = ExitStack()
    with ctx:
        def sb(name, shape, dt=F32):
            return ctx.enter_context(nc.sbuf_tensor(name, shape, dt))

        sems = {}

        def sem(name):
            if name not in sems:
                sems[name] = ctx.enter_context(nc.semaphore(name))
            return sems[name]

        early = sb("early", [P, 3 * U * D])
        x_all = early[:, 0:U * D].rearrange("p (u d) -> p u d", u=U)
        ck_all = early[:, U * D:2 * U * D].rearrange("p (u d) -> p u d", u=U)
        cv_all = early[:, 2 * U * D:3 * U * D].rearrange("p (u d) -> p u d", u=U)
        hs_all = early[:, 0:SLOTS * ROW].rearrange("p (s c) -> p s c", s=SLOTS)
        h_all = sb("h_all", [P, U, D])
        hT_all = sb("hT_all", [P, U, D])
        wup_sb = sb("wup_sb", [P, NE, 2 * I])
        wdn_sb = sb("wdn_sb", [P, NE, CH, D])
        wv_sb = sb("wv_sb", [P, D])
        wo_sb = sb("wo_sb", [P, D])
        rw_sb = sb("rw_sb", [P, E])
        bv_sb = sb("bv_sb", [P, D])
        bo_sb = sb("bo_sb", [P, D])
        rb_sb = sb("rb_sb", [P, E])
        id_sb = sb("id_sb", [P, P])
        hmask_sb = sb("hmask_sb", [P, HG + 2])
        tri_sb = sb("tri_sb", [P, 2, P])
        small_sb = sb("small_sb", [P, U + SLOTS + E])
        thr = small_sb[:, 0:U]
        slot_no = small_sb[:, U:U + SLOTS]
        first_wins = small_sb[:, U + SLOTS:]
        tok_sb = sb("tok_sb", [P, U])
        nowhere_row = sb("nowhere_row", [P, ROW])
        mhalf = sb("mhalf", [P, 1])

        st = {k: sb(f"st_{k}", [P, 6]) for k in "psx"}
        mv = {k: sb(f"mv_{k}", [P, 2]) for k in "psx"}
        ve = {k: sb(f"ve_{k}", [P, 1]) for k in "psx"}
        rs = {k: sb(f"rs_{k}", [P, 1]) for k in "psx"}
        xn = {k: sb(f"xn_{k}", [P, D]) for k in "psx"}
        xnT = sb("xnT", [P, D])
        pn = sb("pn", [P, D])
        pT = sb("pT", [P, G, S])
        q_bd = {"s": [sb(f"q_bd_s{i}", [P, G, P]) for i in range(2)], "x": [sb("q_bd_x", [P, G, P])] * 2}
        k_hd = {k: [sb(f"k_hd_{k}{i}", [P, G, HG, S]) for i in range(2)] for k in "sx"}
        v_bd = {k: [sb(f"v_bd_{k}{i}", [P, VALL]) for i in range(2)] for k in "sx"}
        mx = {k: sb(f"mx_{k}", [P, G, HG]) for k in "sx"}
        pr = {k: sb(f"pr_{k}", [P, G, HG, S]) for k in "sx"}
        prT = {k: sb(f"prT_{k}", [P, G, 4, P]) for k in "sx"}
        rden = {k: sb(f"rden_{k}", [P, HP, 2]) for k in "sx"}
        on = {k: sb(f"on_{k}", [P, HP, 2, DK]) for k in "sx"}
        orow = [sb(f"orow{i}", [P, D]) for i in range(2)]
        onT = sb("onT", [P, D])
        hT = sb("hT", [P, D])
        logits = sb("logits", [P, U, E])

        bank = [ctx.enter_context(nc.psum_tensor(f"bank{i}", [P, 512], F32)) for i in range(8)]
        ps_s = {"s": [bank[0], bank[1]], "x": [bank[2], bank[3]]}
        ps_o = {"s": bank[4], "x": bank[5]}
        ps_xT, ps_p, ps_pT = (bank[6][:, i * P:(i + 1) * P] for i in range(3))
        ps_qT, ps_oT, ps_wo = (bank[7][:, i * P:(i + 1) * P] for i in range(3))
        ps_hT = bank[4][:, 0:P]
        ps_r = bank[5][:, 0:E]

        rowb = [sb(f"rowb{i}", [P, ROW]) for i in range(2)]
        place = [sb(f"place{i}", [P, 1], I32) for i in range(2)]
        token = [sb(f"token{i}", [P, 1], I32) for i in range(2)]
        yrow = [sb(f"yrow{i}", [P, D]) for i in range(2)]
        fx = [sb(f"fx{i}", [P, D]) for i in range(2)]
        fhT = [sb(f"fhT{i}", [P, D]) for i in range(2)]
        gate = [sb(f"gate{i}", [P, I]) for i in range(2)]
        gT = [sb(f"gT{i}", [P, CH, P]) for i in range(2)]
        ps_gate = [bank[0], bank[1]]
        ps_up = [bank[2], bank[3]]
        ps_gT = [bank[4], bank[5]]
        ps_y = [bank[6][:, 0:D], bank[7][:, 0:D]]
        ps_fhT = [bank[4][:, CH * P:], bank[5][:, CH * P:]]
        rt = {n: sb(f"rt_{n}", [P, U, E]) for n in ("l", "cl", "q", "pr", "t", "ml", "key", "eq", "oh")}
        r1 = {n: sb(f"r1_{n}", [P, U]) for n in ("max", "win", "p", "tw", "rtw", "c1", "pos")}
        meta = sb("meta", [P, U, 2])
        et = {n: sb(f"et_{n}", [P, E, U]) for n in ("zero", "incl", "pos", "cmp")}
        e1 = {n: sb(f"e1_{n}", [P, E]) for n in ("n", "tiles", "ctiles", "excl", "shift")}
        se_cmp = sb("se_cmp", [P, SLOTS, E])
        se_f = sb("se_f", [P, SLOTS])
        slot_expert = sb("slot_expert", [P, SLOTS], I32)
        ps_pre = bank[0][:, 0:E * U]
        ps_tot = bank[1][:, 0:E * U]

        load = lambda eng, dst, src, name: eng.dma_start(dst, src).then_inc(sem(name), 16)

        def at(unit):
            return unit + 1

        def steps(eng, body, n, head, tail):
            for t in range(head):
                body(t, t % 2)
            with eng.Fori(0, (n - head - tail) // 2) as i:
                for k in range(2):
                    body(i * 2 + (head + k), (head + k) % 2)
            for t in range(n - tail, n):
                body(t, t % 2)

        DELAY = {"n": 0, "p": 1, "s": 2, "w": 4, "x": 5, "r": 6}
        A_STEPS, A_PEEL, A_LOOP_END = U + 6, 8, U

        def phase_a(eng, body):
            def one(t, par, fixed):
                u = {k: t - d for k, d in DELAY.items()}
                parity = {k: (par - d) % 2 for k, d in DELAY.items()}
                live = lambda k, off=0: not fixed or 0 <= u[k] + off < U
                body(u, parity, live)

            for t in range(A_PEEL):
                one(t, t % 2, True)
            with eng.Fori(0, (A_LOOP_END - A_PEEL) // 2) as i:
                for k in range(2):
                    one(i * 2 + (A_PEEL + k), k % 2, False)
            for t in range(A_LOOP_END, A_STEPS):
                one(t, t % 2, True)

        def wait_apart(eng, *waits):
            waits = [(name, value if isinstance(value, int) else eng.snap(eng.to_reg(value))) for name, value in waits]
            eng.wait_ge(sem("ready"), 1)
            for name, value in waits:
                eng.wait_ge(sem(name), value)

        def early_unit(u):
            return isinstance(u, int) and u < 2

        def first_unit(u):
            return isinstance(u, int) and u < 1

        block = ctx.enter_context(nc.Block())

        o_dram = nc.dram_tensor("attention_out", (U, NB, H, S, DK), F32, kind="Internal").ap()
        o_rows = o_dram.rearrange("u b h q d -> (u b h q d)").rearrange("(u p c) -> u p c", p=P, c=D)
        hs_dram = nc.dram_tensor("sorted_rows", (SLOTS * P, ROW), F32, kind="Internal").ap()
        hs_tiles = hs_dram.rearrange("(s p) c -> p s c", p=P)

        @block.sync
        def _(sp):
            xv = x.rearrange("(u p) d -> p u d", p=P)
            load(sp, x_all[:, 0:4, :], xv[:, 0:4, :], "l_x0")
            load(sp, id_sb[:], ident, "l_small")
            load(sp, wv_sb[:], wv, "l_small")
            load(sp, bv_sb[:], bv.partition_broadcast(P), "l_small")
            load(sp, hmask_sb[:], hmask, "l_small")
            load(sp, wo_sb[:], wo, "l_small")
            load(sp, bo_sb[:], bo.partition_broadcast(P), "l_small")
            load(sp, rw_sb[:], rw, "l_small")
            load(sp, rb_sb[:], rb.partition_broadcast(P), "l_small")
            load(sp, small_sb[:], small.partition_broadcast(P), "l_small")
            load(sp, tok_sb[:], tokens, "l_small")
            load(sp, tri_sb[:], tri, "l_small")
            load(sp, ck_all[:], ctxk, "l_ctx")
            load(sp, cv_all[:], ctxv, "l_ctx")
            load(sp, x_all[:, 4:U, :], xv[:, 4:U, :], "l_x1")
            load(sp, wup_sb[:], wup, "l_w")
            for c in range(CH):
                rows = P if c < CH - 1 else LAST
                load(sp, wdn_sb[0:rows, :, c, :],
                     wdn[:, c * P:c * P + rows, :].rearrange("e i c -> i e c"), "l_w")
            sp.wait_ge(sem("nowhere"), 1)
            load(sp, hs_tiles, nowhere_row[:, :].unsqueeze(1).broadcast_to([P, SLOTS, ROW]), "prefilled")

            def body(u, par, live):
                if live("s"):
                    sp.wait_ge(sem("s_on"), at(u["s"]))
                    for b in range(NB):
                        load(sp, o_dram[u["s"], b, :, :, :].rearrange("h q d -> q h d"),
                             on["s"][S * b:S * (b + 1), :, :, :].rearrange("p a c d -> p (a c) d"), "s_out")
                    wait_apart(sp, ("s_out", 16 * NB * at(u["s"])),
                               *([] if early_unit(u["s"]) else [("s_oT", at(u["s"]) - 2)]))
                    load(sp, orow[par["s"]][:], o_rows[u["s"], :, :], "w_rows")

            phase_a(sp, body)

            for n in range(2):
                sp.wait_ge(sem(f"b_sent{n}"), 16 * (U // 2))
            load(sp, hs_all[:, 0, :], hs_tiles[:, 0, :], "c_row0")
            load(sp, hs_all[:, 1, :], hs_tiles[:, 1, :], "c_row1")
            with sp.Fori(0, (SLOTS - 2) // 2) as i:
                for k in range(2):
                    sp.wait_ge(sem(f"c_row{k}"), i * 16 + 16)
                    load(sp, hs_all[:, i * 2 + (2 + k), :], hs_tiles[:, i * 2 + (2 + k), :], f"c_row{k}")

        N_SMALL = 16 * 11

        ones_in_v = lambda v, h2: v[S * h2:S * (h2 + 1), 0:HP * VW].rearrange(
            "p (a b c d) -> p a b c d", a=HP, b=NB, c=2)[:, :, :, h2, DK:DK + 1]

        def v_slots(v, h2):
            return v[S * h2:S * (h2 + 1), 0:HP * VW].rearrange(
                "p (a b c d) -> p a b c d", a=HP, b=NB, c=2)[:, :, :, h2, 0:DK]

        @block.gpsimd
        def _(pool):
            nc.gpsimd.memset(nowhere_row[:, 0:TOK], 0.0)
            nc.gpsimd.memset(nowhere_row[:, TOK:ROW], NOWHERE).then_inc(sem("nowhere"), 1)
            nc.gpsimd.memset(mhalf[:], -0.5).then_inc(sem("ready"), 1)
            for i in range(2):
                nc.gpsimd.memset(q_bd["s"][i][:], 0.0)
            nc.gpsimd.memset(q_bd["x"][0][:], 0.0).then_inc(sem("zeros"), 1)
            for k in "sx":
                for i in range(2):
                    nc.gpsimd.memset(v_bd[k][i][:], 0.0).then_inc(sem("v_zero"), 1)
            pool.wait_ge(sem("v_zero"), 4)
            for k in "sx":
                for i in range(2):
                    for h2 in range(2):
                        nc.gpsimd.memset(ones_in_v(v_bd[k][i], h2), 1.0).then_inc(sem("v_ones"), 1)
            pool.wait_ge(sem("v_ones"), 8)
            pool.wait_ge(sem("ready"), 1)
            pool.wait_ge(sem("l_small"), N_SMALL)
            pool.wait_ge(sem("l_ctx"), 32)

            def rstd(k, u):
                pool.wait_ge(sem(f"{k}_ve"), at(u))
                nc.gpsimd.tensor_tensor(rs[k][:], ve[k][:], mhalf[:], ALU.pow).then_inc(sem(f"{k}_rs"), 1)

            def by_head(k, par, src, u):
                if not early_unit(u):
                    pool.wait_ge(sem(f"{k}_sc"), at(u) * 2 - 4)
                nc.gpsimd.tensor_tensor(
                    k_hd[k][par][:], src.unsqueeze(2).broadcast_to([P, G, HG, S]),
                    hmask_sb[:, 0:HG].unsqueeze(1).unsqueeze(3).broadcast_to([P, G, HG, S]),
                    ALU.mult).then_inc(sem(f"{k}_khd"), 1)

            def body(u, par, live):
                if live("r"):
                    rstd("x", u["r"])
                if live("w"):
                    by_head("x", par["w"], ck_all[:, u["w"], :].rearrange("p (g k) -> p g k", g=G), u["w"])
                    if not early_unit(u["w"]):
                        wait_apart(pool, ("x_pv", at(u["w"]) * 2 - 4))
                    nc.gpsimd.tensor_tensor(
                        v_bd["x"][par["w"]][:, 0:HP * VW].rearrange("p (a c d) -> p a c d", c=2, d=DK + 1)[:, :, :, 0:DK],
                        cv_all[:, u["w"], :].rearrange("p (a d) -> p a d", d=DK).unsqueeze(2).broadcast_to([P, HP * NB, 2, DK]),
                        hmask_sb[:, HG:HG + 2].unsqueeze(1).unsqueeze(3).broadcast_to([P, HP * NB, 2, DK]),
                        ALU.mult).then_inc(sem("x_v"), 1)
                    rstd("s", u["w"])
                if live("p"):
                    pool.wait_ge(sem("p_pT"), at(u["p"]))
                    by_head("s", par["p"], pT[:, :, :], u["p"])
                    pool.wait_ge(sem("p_xn"), at(u["p"]))
                    nc.gpsimd.tensor_tensor(x_all[:, u["p"], :], x_all[:, u["p"], :], bo_sb[:], ALU.add).then_inc(sem("p_xb"), 1)
                if live("r"):
                    wait_apart(pool, ("x_xn", at(u["r"])))
                    nc.gpsimd.tensor_copy(h_all[:, u["r"], :], xn["x"][:]).then_inc(sem("x_h"), 1)
                if live("n"):
                    rstd("p", u["n"])

            phase_a(pool, body)

            pool.wait_ge(sem("prefilled"), 16)

            def send(n, p):
                wait_apart(pool, ("f_y", at(n)))
                pool.indirect_dma_start(
                    out=hs_dram, out_offset=bass.IndirectOffsetOnAxis(ap=place[p][:, 0:1], axis=0),
                    in_=rowb[p][:, :], in_offset=None).then_inc(sem(f"b_sent{p}"), 16)

            steps(pool, send, U, 0, 0)

            def put(s, p):
                wait_apart(pool, ("f_y", at(s + U)))
                pool.indirect_dma_start(
                    out=out, out_offset=bass.IndirectOffsetOnAxis(ap=token[p][:, 0:1], axis=0),
                    in_=yrow[p][:, :], in_offset=None,
                    bounds_check=NTOK - 1, oob_is_err=False).then_inc(sem(f"c_put{p}"), 16)

            steps(pool, put, SLOTS, 0, 0)
            for n in range(2):
                pool.wait_ge(sem(f"c_put{n}"), 16 * (SLOTS // 2))

        @block.tensor
        def _(pe):
            pe.wait_ge(sem("l_small"), N_SMALL)
            pe.wait_ge(sem("zeros"), 1)
            pe.wait_ge(sem("v_ones"), 8)

            def scores(k, par, u, g):
                if g == 0:
                    pe.wait_ge(sem(f"{k}_khd"), at(u))
                    pe.wait_ge(sem(f"{k}_qbd"), at(u))
                if not first_unit(u):
                    pe.wait_ge(sem(f"{k}_prT{g}"), at(u) - 1)
                nc.tensor.matmul(ps_s[k][g][:, :], q_bd[k][par][:, g, :],
                                 k_hd[k][par][:, g, :, :].rearrange("p h k -> p (h k)"),
                                 start=True, stop=True).then_inc(sem(f"{k}_sc"), 1)

            def turn(k, u, g):
                pe.wait_ge(sem(f"{k}_exp{g}"), at(u))
                for i in range(4):
                    last = nc.tensor.transpose(ps_s[k][g][:, i * P:(i + 1) * P],
                                               pr[k][:, g, 2 * i:2 * i + 2, :].rearrange("p h k -> p (h k)"), id_sb[:])
                last.then_inc(sem(f"{k}_turn{g}"), 1)

            def weigh(k, par, u, g):
                pe.wait_ge(sem(f"{k}_prT{g}"), at(u))
                if g == 0:
                    pe.wait_ge(sem(f"{k}_v"), at(u))
                    if not first_unit(u):
                        pe.wait_ge(sem(f"{k}_on"), at(u) - 1)
                    if k == "s" and not (isinstance(u, int) and u < 4):
                        pe.wait_ge(sem("r_hTall"), at(u) - 4)
                    if k == "x" and not first_unit(u):
                        pe.wait_ge(sem("r_log"), at(u) - 1)
                for i in range(4):
                    at_col = (4 * g + i) * VW
                    last = nc.tensor.matmul(ps_o[k][:, at_col:at_col + P], prT[k][:, g, i, :],
                                            v_bd[k][par][:, at_col:at_col + P], start=True, stop=True)
                last.then_inc(sem(f"{k}_pv"), 1)

            def body(u, par, live):
                if live("x"):
                    pe.wait_ge(sem("s_xn"), at(u["x"]))
                    nc.tensor.transpose(ps_qT, xn["s"][:], id_sb[:]).then_inc(sem("s_qT"), 1)
                if live("p"):
                    pe.wait_ge(sem("p_xn"), at(u["p"]))
                    if not first_unit(u["p"]):
                        pe.wait_ge(sem("p_pT"), at(u["p"]) - 1)
                    nc.tensor.transpose(ps_xT, xn["p"][:], id_sb[:]).then_inc(sem("p_xT"), 1)
                if live("s"):
                    scores("s", par["s"], u["s"], 0)
                if live("p"):
                    pe.wait_ge(sem("p_xnT"), at(u["p"]))
                    nc.tensor.matmul(ps_p, xnT[:], wv_sb[:], start=True, stop=True).then_inc(sem("p_p"), 1)
                if live("w"):
                    pe.wait_ge(sem("w_rows"), at(u["w"]) * 16)
                    if not first_unit(u["w"]):
                        pe.wait_ge(sem("x_qbd"), at(u["w"]) - 1)
                    nc.tensor.transpose(ps_oT, orow[par["w"]][:], id_sb[:]).then_inc(sem("s_oT"), 1)
                if live("s"):
                    scores("s", par["s"], u["s"], 1)
                if live("w"):
                    pe.wait_ge(sem("s_onT"), at(u["w"]))
                    nc.tensor.matmul(ps_wo, onT[:], wo_sb[:], start=True, stop=True).then_inc(sem("s_wo"), 1)
                if live("x"):
                    scores("x", par["x"], u["x"], 0)
                if live("p"):
                    pe.wait_ge(sem("p_pn"), at(u["p"]))
                    nc.tensor.transpose(ps_pT, pn[:], id_sb[:]).then_inc(sem("p_T"), 1)
                if live("x"):
                    scores("x", par["x"], u["x"], 1)
                if live("r"):
                    pe.wait_ge(sem("x_xn"), at(u["r"]))
                    pe.wait_ge(sem("s_on"), min(at(u["r"]) + 3, U) if isinstance(u["r"], int) else at(u["r"]) + 3)
                    nc.tensor.transpose(ps_hT, xn["x"][:], id_sb[:]).then_inc(sem("r_hT"), 1)
                if live("s"):
                    turn("s", u["s"], 0)
                    turn("s", u["s"], 1)
                if live("s"):
                    weigh("s", par["s"], u["s"], 0)
                    weigh("s", par["s"], u["s"], 1)
                if live("r"):
                    pe.wait_ge(sem("r_hTs"), at(u["r"]))
                    nc.tensor.matmul(ps_r, hT[:], rw_sb[:], start=True, stop=True).then_inc(sem("r_r"), 1)
                if live("x"):
                    turn("x", u["x"], 0)
                    turn("x", u["x"], 1)
                    weigh("x", par["x"], u["x"], 0)
                    weigh("x", par["x"], u["x"], 1)

            phase_a(pe, body)

            pe.wait_ge(sem("chosen"), 1)
            by_et = rt["oh"][:].rearrange("p u e -> p e u")
            nc.tensor.matmul(ps_pre, tri_sb[:, 0, :], by_et, start=True, stop=True)
            nc.tensor.matmul(ps_tot, tri_sb[:, 1, :], by_et, start=True, stop=True).then_inc(sem("counted"), 1)
            pe.wait_ge(sem("placed"), 1)
            pe.wait_ge(sem("l_w"), 16 * (1 + CH))

            def up(n, p, expert):
                if not early_unit(n):
                    pe.wait_ge(sem("f_act"), at(n) - 2)
                    pe.wait_ge(sem("f_g"), at(n) - 2)
                pe.wait_ge(sem("f_hT"), at(n))
                nc.tensor.matmul(ps_gate[p][:, 0:I], fhT[p][:], wup_sb[:, expert, 0:I],
                                 start=True, stop=True).then_inc(sem("f_gate"), 1)
                nc.tensor.matmul(ps_up[p][:, 0:I], fhT[p][:], wup_sb[:, expert, I:2 * I],
                                 start=True, stop=True).then_inc(sem("f_up"), 1)

            def turn_g(n, p):
                pe.wait_ge(sem("f_g"), at(n))
                if not early_unit(n):
                    pe.wait_ge(sem("f_gT"), at(n) - 2)
                for c in range(CH):
                    w = P if c < CH - 1 else LAST
                    last = nc.tensor.transpose(ps_gT[p][0:w, c * P:(c + 1) * P], gate[p][:, c * P:c * P + w], id_sb[:])
                last.then_inc(sem("f_turn"), 1)

            def down(n, p, expert):
                pe.wait_ge(sem("f_gT"), at(n))
                if not early_unit(n):
                    pe.wait_ge(sem("f_y"), at(n) - 2)
                for c in range(CH):
                    w = P if c < CH - 1 else LAST
                    last = nc.tensor.matmul(ps_y[p], gT[p][0:w, c, :], wdn_sb[0:w, expert, c, :],
                                            start=(c == 0), stop=(c == CH - 1))
                last.then_inc(sem("f_down"), 1)

            def shared(n, p):
                if not (isinstance(n, int) and n + 1 >= U):
                    up(n + 1, 1 - p, E)
                if not first_unit(n):
                    down(n - 1, 1 - p, E)
                turn_g(n, p)

            up(0, 0, E)
            steps(pe, shared, U, 3, 1)
            down(U - 1, (U - 1) % 2, E)

            def expert_of(s):
                return pe.value_load(slot_expert[0:1, s:s + 1] if isinstance(s, int) else slot_expert[0:1, bass.ds(s, 1)],
                                     min_val=0, max_val=E - 1)

            def to_hT(s, p):
                pe.wait_ge(sem("c_fx"), at(s))
                pe.wait_ge(sem("f_gT"), U if isinstance(s, int) and s < 3 else at(s + U) - 4)
                if not early_unit(s):
                    pe.wait_ge(sem("f_hT"), at(s + U) - 2)
                nc.tensor.transpose(ps_fhT[p], fx[p][:], id_sb[:]).then_inc(sem("c_hT"), 1)

            def routed(s, p):
                tail = isinstance(s, int)
                if not (tail and s + 1 >= SLOTS):
                    up(s + (U + 1), 1 - p, expert_of(s + 1))
                if not (tail and s + 3 >= SLOTS):
                    to_hT(s + 3, 1 - p)
                if not first_unit(s):
                    down(s + (U - 1), 1 - p, expert_of(s - 1))
                pe.wait_ge(sem("f_hT"), min(at(s + U) + 2, U + SLOTS) if tail else at(s + U) + 2)
                turn_g(s + U, p)

            to_hT(0, 0)
            to_hT(1, 1)
            up(U, 0, expert_of(0))
            to_hT(2, 0)
            steps(pe, routed, SLOTS, 2, 4)
            down(U + SLOTS - 1, (SLOTS - 1) % 2, expert_of(SLOTS - 1))

        @block.scalar
        def _(act):
            act.wait_ge(sem("zeros"), 1)

            def block_diagonal(k, par, u, src, wait):
                act.wait_ge(sem(wait), at(u))
                if k == "s":
                    if not early_unit(u):
                        act.wait_ge(sem("s_sc"), at(u) * 2 - 4)
                elif not first_unit(u):
                    act.wait_ge(sem("x_sc"), at(u) * 2 - 2)
                for g in range(G):
                    for b in range(NB):
                        last = nc.scalar.copy(q_bd[k][par][S * b:S * (b + 1), g, S * b:S * (b + 1)],
                                              src[S * g:S * (g + 1), S * b:S * (b + 1)])
                last.then_inc(sem(f"{k}_qbd"), 1)

            def exp(k, u, g):
                act.wait_ge(sem(f"{k}_sub{g}"), at(u))
                nc.scalar.activation(pr[k][:, g, :, :], pr[k][:, g, :, :], ACT.Exp,
                                     scale=float(DK) ** -0.5).then_inc(sem(f"{k}_exp{g}"), 1)

            def turned(k, u, g):
                act.wait_ge(sem(f"{k}_turn{g}"), at(u))
                if not first_unit(u):
                    act.wait_ge(sem(f"{k}_pv"), 2 * at(u) - 3 + g)
                nc.scalar.copy(prT[k][:, g, :, :].rearrange("p i q -> p (i q)"), ps_s[k][g][:, :]).then_inc(sem(f"{k}_prT{g}"), 1)

            def body(u, par, live):
                if live("x"):
                    block_diagonal("x", par["x"], u["x"], ps_qT, "s_qT")
                if live("p"):
                    act.wait_ge(sem("p_xT"), at(u["p"]))
                    nc.scalar.copy(xnT[:], ps_xT).then_inc(sem("p_xnT"), 1)
                if live("w"):
                    act.wait_ge(sem("s_oT"), at(u["w"]))
                    nc.scalar.copy(onT[:], ps_oT).then_inc(sem("s_onT"), 1)
                if live("s"):
                    exp("s", u["s"], 0)
                if live("p"):
                    act.wait_ge(sem("p_pn"), at(u["p"]))
                    if not early_unit(u["p"]):
                        act.wait_ge(sem("s_pv"), at(u["p"]) * 2 - 4)
                    for b in range(NB):
                        for h2 in range(2):
                            src = pn[S * b:S * (b + 1), :].rearrange("p (a c d) -> p a c d", a=HP, c=2)[:, :, h2, :]
                            last = nc.scalar.copy(v_slots(v_bd["s"][par["p"]], h2)[:, :, b, :], src)
                    last.then_inc(sem("s_v"), 1)
                if live("s"):
                    exp("s", u["s"], 1)
                if live("p"):
                    block_diagonal("s", par["p"], u["p"], ps_pT, "p_T")
                    if not first_unit(u["p"]):
                        act.wait_ge(sem("s_khd"), at(u["p"]) - 1)
                    for g in range(G):
                        for b in range(NB):
                            last = nc.scalar.copy(pT[S * b:S * (b + 1), g, :], ps_pT[S * g:S * (g + 1), S * b:S * (b + 1)])
                    last.then_inc(sem("p_pT"), 1)
                if live("r"):
                    act.wait_ge(sem("r_hT"), at(u["r"]))
                    nc.scalar.copy(hT[:], ps_hT).then_inc(sem("r_hTs"), 1)
                    nc.scalar.copy(hT_all[:, u["r"], :], ps_hT).then_inc(sem("r_hTall"), 1)
                if live("s"):
                    turned("s", u["s"], 0)
                    turned("s", u["s"], 1)
                if live("x"):
                    exp("x", u["x"], 0)
                if live("x"):
                    exp("x", u["x"], 1)
                    turned("x", u["x"], 0)
                    turned("x", u["x"], 1)

            phase_a(act, body)

            act.wait_ge(sem("clipped"), 1)
            nc.scalar.activation(rt["q"][:], rt["cl"][:], ACT.Exp, scale=-1.0).then_inc(sem("exped"), 1)

            def silu(n, p):
                act.wait_ge(sem("f_gate"), at(n))
                if not early_unit(n):
                    act.wait_ge(sem("f_turn"), at(n) - 2)
                nc.scalar.activation(gate[p][:], ps_gate[p][:, 0:I], ACT.Silu).then_inc(sem("f_act"), 1)

            def gate_turned(n, p):
                act.wait_ge(sem("f_turn"), at(n))
                if not early_unit(n):
                    act.wait_ge(sem("f_down"), at(n) - 2)
                nc.scalar.copy(gT[p][:, 0:CH - 1, :].rearrange("p c q -> p (c q)"), ps_gT[p][:, 0:(CH - 1) * P])
                nc.scalar.copy(gT[p][0:LAST, CH - 1, :], ps_gT[p][0:LAST, (CH - 1) * P:CH * P]).then_inc(sem("f_gT"), 1)

            def copy_hT(n, p):
                if not early_unit(n):
                    act.wait_ge(sem("f_up"), at(n) - 2)
                nc.scalar.copy(fhT[p][:], hT_all[:, n, :]).then_inc(sem("f_hT"), 1)

            def shared(n, p):
                if not (isinstance(n, int) and n + 1 >= U):
                    silu(n + 1, 1 - p)
                if not (isinstance(n, int) and n + 3 >= U):
                    copy_hT(n + 3, 1 - p)
                gate_turned(n, p)

            act.wait_ge(sem("r_hTall"), U)
            copy_hT(0, 0)
            copy_hT(1, 1)
            silu(0, 0)
            copy_hT(2, 0)
            steps(act, shared, U, 3, 3)

            def routed_hT(s, p):
                act.wait_ge(sem("c_hT"), at(s))
                act.wait_ge(sem("f_up"), at(s + U) - 2)
                nc.scalar.copy(fhT[p][:], ps_fhT[p]).then_inc(sem("f_hT"), 1)

            def routed(s, p):
                if not (isinstance(s, int) and s + 1 >= SLOTS):
                    silu(s + (U + 1), 1 - p)
                if not (isinstance(s, int) and s + 3 >= SLOTS):
                    routed_hT(s + 3, 1 - p)
                gate_turned(s + U, p)

            routed_hT(0, 0)
            routed_hT(1, 1)
            silu(U, 0)
            routed_hT(2, 0)
            steps(act, routed, SLOTS, 3, 3)

        @block.vector
        def _(dve):
            done = [0]

            def link(ins):
                done[0] += 1
                ins.then_inc(sem("chain"), 1)
                dve.wait_ge(sem("chain"), done[0])

            def stats(k, src, u):
                nc.vector.bn_stats(st[k][:], src).then_inc(sem(f"{k}_st"), 1)
                wait_apart(dve, (f"{k}_st", at(u)))
                nc.vector.bn_aggr(mv[k][:], st[k][:]).then_inc(sem(f"{k}_mv"), 1)
                dve.wait_ge(sem(f"{k}_mv"), at(u))
                nc.vector.tensor_scalar(ve[k][:], mv[k][:, 1:2], EPS, None, ALU.add).then_inc(sem(f"{k}_ve"), 1)

            def normed(k, src, u):
                dve.wait_ge(sem(f"{k}_rs"), at(u))
                nc.vector.tensor_scalar(xn[k][:], src, mv[k][:, 0:1], rs[k][:, 0:1], ALU.subtract, ALU.mult).then_inc(sem(f"{k}_xn"), 1)

            def soften(k, u, g):
                dve.wait_ge(sem(f"{k}_sc"), 2 * at(u) - 1 + g)
                sc = ps_s[k][g][:, :].rearrange("p (h k) -> p h k", h=HG)
                nc.vector.tensor_reduce(mx[k][:, g, :], sc, AX.X, ALU.max).then_inc(sem(f"{k}_mx"), 1)
                dve.wait_ge(sem(f"{k}_mx"), 2 * at(u) - 1 + g)
                if not first_unit(u):
                    dve.wait_ge(sem(f"{k}_turn{g}"), at(u) - 1)
                nc.vector.tensor_tensor(pr[k][:, g, :, :], sc, mx[k][:, g, :].unsqueeze(2).broadcast_to([P, HG, S]),
                                        ALU.subtract).then_inc(sem(f"{k}_sub{g}"), 1)

            def normalise(k, u):
                dve.wait_ge(sem(f"{k}_pv"), 2 * at(u))
                o = [ps_o[k][S * b:S * (b + 1), 0:HP * VW].rearrange("p (a b c d) -> p a b c d", a=HP, b=NB, c=2)[:, :, b, :, :]
                     for b in range(NB)]
                for b in range(NB):
                    last = nc.vector.reciprocal(rden[k][S * b:S * (b + 1), :, :], o[b][:, :, :, DK])
                last.then_inc(sem(f"{k}_rden"), 1)
                dve.wait_ge(sem(f"{k}_rden"), at(u))
                if k == "s" and not first_unit(u):
                    dve.wait_ge(sem("s_out"), 16 * NB * (at(u) - 1))
                for b in range(NB):
                    rows = slice(S * b, S * (b + 1))
                    last = nc.vector.tensor_tensor(on[k][rows, :, :, :], o[b][:, :, :, 0:DK],
                                                   rden[k][rows, :, :].unsqueeze(3).broadcast_to([S, HP, 2, DK]), ALU.mult)
                last.then_inc(sem(f"{k}_on"), 1)

            def body(u, par, live):
                if live("s"):
                    soften("s", u["s"], 0)
                if live("p"):
                    dve.wait_ge(sem("p_p"), at(u["p"]))
                    if not first_unit(u["p"]):
                        dve.wait_ge(sem("p_T"), at(u["p"]) - 1)
                        dve.wait_ge(sem("s_v"), at(u["p"]) - 1)
                    nc.vector.tensor_tensor(pn[:], ps_p, bv_sb[:], ALU.add).then_inc(sem("p_pn"), 1)
                if live("r"):
                    if not first_unit(u["r"]):
                        dve.wait_ge(sem("r_hT"), at(u["r"]) - 1)
                        dve.wait_ge(sem("x_h"), at(u["r"]) - 1)
                    normed("x", x_all[:, u["r"], :], u["r"])
                if live("w"):
                    xs = x_all[:, u["w"], :]
                    dve.wait_ge(sem("p_xb"), at(u["w"]))
                    dve.wait_ge(sem("s_wo"), at(u["w"]))
                    nc.vector.tensor_tensor(xs, ps_wo, xs, ALU.add).then_inc(sem("s_x"), 1)
                if live("s"):
                    soften("s", u["s"], 1)
                if live("w"):
                    wait_apart(dve, ("s_x", at(u["w"])))
                    stats("s", xs, u["w"])
                if live("x"):
                    soften("x", u["x"], 0)
                if live("w"):
                    if not first_unit(u["w"]):
                        dve.wait_ge(sem("s_qT"), at(u["w"]) - 1)
                    normed("s", xs, u["w"])
                if live("x"):
                    soften("x", u["x"], 1)
                if live("n"):
                    stats("p", x_all[:, u["n"], :], u["n"])
                if live("s"):
                    normalise("s", u["s"])
                if live("r"):
                    dve.wait_ge(sem("r_r"), at(u["r"]))
                    nc.vector.tensor_copy(logits[:, u["r"], :], ps_r).then_inc(sem("r_log"), 1)
                if live("n"):
                    if not first_unit(u["n"]):
                        dve.wait_ge(sem("p_xT"), at(u["n"]) - 1)
                    normed("p", x_all[:, u["n"], :], u["n"])
                if live("x"):
                    normalise("x", u["x"])
                    xx = x_all[:, u["x"], :]
                    dve.wait_ge(sem("x_on"), at(u["x"]))
                    nc.vector.tensor_tensor(xx, xx, on["x"][:].rearrange("p a b d -> p (a b d)"), ALU.add).then_inc(sem("x_x"), 1)
                    wait_apart(dve, ("x_x", at(u["x"])))
                    stats("x", xx, u["x"])

            dve.wait_ge(sem("l_small"), N_SMALL)
            dve.wait_ge(sem("l_x0"), 16)
            dve.wait_ge(sem("l_x1"), 16)
            phase_a(dve, body)

            bce = lambda a: a.unsqueeze(2).broadcast_to([P, U, E])
            bcu = lambda a: a.unsqueeze(1).broadcast_to([P, U, E])
            dve.wait_ge(sem("r_log"), U)
            link(nc.vector.tensor_tensor(rt["l"][:], logits[:], bcu(rb_sb[:, :]), ALU.add))
            nc.vector.tensor_scalar(rt["cl"][:], rt["l"][:], -50.0, 50.0, ALU.max, ALU.min).then_inc(sem("clipped"), 1)
            dve.wait_ge(sem("exped"), 1)
            link(nc.vector.tensor_scalar(rt["q"][:], rt["q"][:], 1.0, None, ALU.add))
            nc.vector.reciprocal(rt["pr"][:], rt["q"][:])
            nc.vector.tensor_scalar(rt["ml"][:], rt["cl"][:], KNEE, None, ALU.min)
            link(nc.vector.tensor_scalar(rt["t"][:], rt["q"][:], Q_KNEE, Q_KNEE, ALU.min, ALU.subtract))
            link(nc.vector.scalar_tensor_tensor(rt["key"][:], rt["t"][:], -8.0, rt["ml"][:], ALU.mult, ALU.add))
            link(nc.vector.tensor_reduce(r1["max"][:], rt["key"][:], AX.X, ALU.max))
            link(nc.vector.tensor_tensor(rt["eq"][:], rt["key"][:], bce(r1["max"][:, :]), ALU.is_ge))
            link(nc.vector.tensor_tensor(rt["t"][:], rt["eq"][:], bcu(first_wins), ALU.mult))
            link(nc.vector.tensor_reduce(r1["win"][:], rt["t"][:], AX.X, ALU.max))
            nc.vector.tensor_tensor(rt["oh"][:], rt["t"][:], bce(r1["win"][:, :]), ALU.is_equal).then_inc(sem("chosen"), 1)
            dve.wait_ge(sem("chosen"), 1)
            link(nc.vector.tensor_tensor(rt["pr"][:], rt["pr"][:], rt["oh"][:], ALU.mult))
            link(nc.vector.tensor_reduce(r1["p"][:], rt["pr"][:], AX.X, ALU.add))
            link(nc.vector.tensor_scalar(r1["p"][:], r1["p"][:], 1e-8, 1.0 - 1e-8, ALU.max, ALU.min))
            link(nc.vector.tensor_scalar(r1["tw"][:], r1["p"][:], 0.5, 1e-8, ALU.add, ALU.add))
            link(nc.vector.tensor_scalar(r1["tw"][:], r1["tw"][:], 0.5, 2.0, ALU.max, ALU.min))
            link(nc.vector.reciprocal(r1["rtw"][:], r1["tw"][:]))
            nc.vector.tensor_scalar(r1["c1"][:], r1["rtw"][:], 0.5, None, ALU.mult)
            link(nc.vector.tensor_tensor(meta[:, :, 0], r1["rtw"][:], r1["p"][:], ALU.mult))
            nc.vector.tensor_copy(meta[:, :, 1], tok_sb[:])
            nc.vector.memset(et["zero"][:], 0.0)
            dve.wait_ge(sem("counted"), 1)
            flat = lambda a: a.rearrange("p e u -> p (e u)")
            tot = ps_tot.rearrange("p (e u) -> p e u", e=E)
            link(nc.vector.tensor_reduce(e1["n"][:], tot, AX.X, ALU.add))
            link(nc.vector.tensor_tensor_scan(flat(et["incl"][:]), ps_tot, flat(et["zero"][:]), 0.0, ALU.add, ALU.add))
            link(nc.vector.tensor_tensor(et["cmp"][:], e1["n"][:, :].unsqueeze(2).broadcast_to([P, E, U]),
                                         thr.unsqueeze(1).broadcast_to([P, E, U]), ALU.is_gt))
            link(nc.vector.tensor_reduce(e1["tiles"][:], et["cmp"][:], AX.X, ALU.add))
            link(nc.vector.tensor_tensor_scan(e1["ctiles"][:], e1["tiles"][:], et["zero"][:, 0, 0:E], 0.0, ALU.add, ALU.add))
            link(nc.vector.tensor_tensor(e1["shift"][:], e1["ctiles"][:], e1["tiles"][:], ALU.subtract))
            link(nc.vector.tensor_tensor(e1["excl"][:], et["incl"][:, :, U - 1], e1["n"][:], ALU.subtract))
            link(nc.vector.scalar_tensor_tensor(e1["shift"][:], e1["shift"][:], float(P), e1["excl"][:], ALU.mult, ALU.subtract))
            link(nc.vector.tensor_tensor(flat(et["pos"][:]), flat(et["incl"][:]), ps_tot, ALU.subtract))
            link(nc.vector.tensor_tensor(flat(et["pos"][:]), flat(et["pos"][:]), ps_pre, ALU.add))
            link(nc.vector.tensor_tensor(et["pos"][:], et["pos"][:], e1["shift"][:, :].unsqueeze(2).broadcast_to([P, E, U]), ALU.add))
            link(nc.vector.tensor_tensor(et["pos"][:], et["pos"][:], rt["oh"][:].rearrange("p u e -> p e u"), ALU.mult))
            link(nc.vector.tensor_reduce(r1["pos"][:], et["pos"][:].rearrange("p e u -> p u e"), AX.X, ALU.add))
            link(nc.vector.tensor_tensor(se_cmp[:], slot_no.unsqueeze(2).broadcast_to([P, SLOTS, E]),
                                         e1["ctiles"][:, :].unsqueeze(1).broadcast_to([P, SLOTS, E]), ALU.is_ge))
            link(nc.vector.tensor_reduce(se_f[:], se_cmp[:], AX.X, ALU.add))
            nc.vector.tensor_scalar(slot_expert[:], se_f[:], float(E - 1), None, ALU.min).then_inc(sem("placed"), 1)

            def gated(n, p):
                dve.wait_ge(sem("f_act"), at(n))
                dve.wait_ge(sem("f_up"), at(n))
                nc.vector.tensor_tensor(gate[p][:], gate[p][:], ps_up[p][:, 0:I], ALU.mult).then_inc(sem("f_g"), 1)

            def shared_row(n, p, sent):
                if sent is not None:
                    dve.wait_ge(sem(f"b_sent{p}"), sent)
                nc.vector.tensor_copy(rowb[p][:, 0:D], h_all[:, n, :])
                nc.vector.tensor_copy(rowb[p][:, WT:ROW], meta[:, n, :])
                nc.vector.tensor_copy(place[p][:], r1["pos"][:, n:n + 1] if isinstance(n, int) else r1["pos"][:, bass.ds(n, 1)])
                dve.wait_ge(sem("f_down"), at(n))
                nc.vector.scalar_tensor_tensor(
                    rowb[p][:, D:2 * D], ps_y[p], r1["c1"][:, n:n + 1] if isinstance(n, int) else r1["c1"][:, bass.ds(n, 1)],
                    x_all[:, n, :], ALU.mult, ALU.add).then_inc(sem("f_y"), 1)
                dve.wait_ge(sem("f_y"), at(n))

            def b_step(n, p, sent):
                if not (isinstance(n, int) and n + 1 >= U):
                    gated(n + 1, 1 - p)
                if not first_unit(n):
                    shared_row(n - 1, 1 - p, sent)

            dve.wait_ge(sem("placed"), 1)
            dve.wait_ge(sem("x_h"), U)
            gated(0, 0)
            PEEL = 4
            for n in range(PEEL):
                b_step(n, n % 2, 16 * ((n - 1) // 2) if n >= 3 else None)
            with dve.Fori(0, (U - PEEL - 2) // 2) as i:
                for k in range(2):
                    b_step(i * 2 + (PEEL + k), k, i * 16 + 16 * ((PEEL + k - 1) // 2))
            for n in range(U - 2, U):
                b_step(n, n % 2, 16 * ((n - 1) // 2))
            shared_row(U - 1, (U - 1) % 2, 16 * ((U - 1) // 2))

            def routed_in(s, p, landed):
                dve.wait_ge(sem(f"c_row{p}"), landed)
                if not early_unit(s):
                    dve.wait_ge(sem("c_hT"), at(s) - 2)
                nc.vector.tensor_copy(fx[p][:], hs_all[:, s, 0:D]).then_inc(sem("c_fx"), 1)

            def routed_row(s, p, put):
                if put is not None:
                    dve.wait_ge(sem(f"c_put{p}"), put)
                nc.vector.tensor_copy(token[p][:], hs_all[:, s, TOK:ROW])
                dve.wait_ge(sem("f_down"), at(s + U))
                nc.vector.scalar_tensor_tensor(yrow[p][:], ps_y[p], hs_all[:, s, WT:WT + 1], hs_all[:, s, D:2 * D],
                                               ALU.mult, ALU.add).then_inc(sem("f_y"), 1)
                dve.wait_ge(sem("f_y"), at(s + U))

            def c_step(s, p, landed, put):
                if not (isinstance(s, int) and s + 1 >= SLOTS):
                    gated(s + (U + 1), 1 - p)
                if landed is not None:
                    routed_in(s + 4, p, landed)
                if not first_unit(s):
                    routed_row(s - 1, 1 - p, put)

            for s in range(3):
                routed_in(s, s % 2, 16 * (s // 2 + 1))
            gated(U, 0)
            routed_in(3, 1, 32)
            for s in range(PEEL):
                c_step(s, s % 2, 16 * ((s + 4) // 2 + 1), 16 * ((s - 1) // 2) if s >= 3 else None)
            with dve.Fori(0, (SLOTS - 4 - PEEL) // 2) as i:
                for k in range(2):
                    c_step(i * 2 + (PEEL + k), k, i * 16 + 16 * ((PEEL + k + 4) // 2 + 1), i * 16 + 16 * ((PEEL + k - 1) // 2))
            for s in range(SLOTS - 4, SLOTS):
                c_step(s, s % 2, None, 16 * ((s - 1) // 2))
            routed_row(SLOTS - 1, (SLOTS - 1) % 2, 16 * ((SLOTS - 1) // 2))


def kernel(**inputs):
    import numpy as np
    import concourse.bacc as bacc
    from concourse.bass_utils import run_bass_kernel_spmd

    a = {k: np.asarray(v) for k, v in inputs.items()}
    f32 = np.float32
    c = a["ctx_1024"]
    p = np.arange(P)
    arrays = {
        "x": a["x"].reshape(NTOK, D),
        "ctxk": c.reshape(U, NB, S, G, HG * DK).transpose(1, 4, 0, 3, 2).reshape(P, U, D),
        "ctxv": c.reshape(U, NB, S, HP, 2, DK).transpose(4, 2, 0, 3, 1, 5).reshape(P, U, D),
        "wv": a["L0_attn_Wv"].T, "bv": a["L0_attn_bv"], "wo": a["L0_attn_Wo"].T, "bo": a["L0_attn_bo"],
        "rw": a["L0_ffn_router_w"].T, "rb": a["L0_ffn_routing_bias"],
        "wup": np.concatenate([np.concatenate([a["L0_ffn_ew1"], a["L0_ffn_sw1"][None]]),
                               np.concatenate([a["L0_ffn_ew3"], a["L0_ffn_sw3"][None]])], axis=1).transpose(2, 0, 1),
        "wdn": np.concatenate([a["L0_ffn_ew2"], a["L0_ffn_sw2"][None]]).transpose(0, 2, 1),
        "ident": np.eye(P, dtype=f32),
        "hmask": np.concatenate([(p[:, None] // DK) % HG == np.arange(HG)[None],
                                 p[:, None] // S == np.arange(2)[None]], axis=1).astype(f32),
        "tri": np.stack([np.triu(np.ones((P, P), f32), 1), np.ones((P, P), f32)], axis=1),
        "small": np.concatenate([np.arange(U) * P, np.arange(SLOTS), E - np.arange(E)]).astype(f32),
        "tokens": (p[:, None] + P * np.arange(U)[None]).astype(f32),
    }
    arrays = {f"in_{k}": np.ascontiguousarray(v) for k, v in arrays.items()}
    nc = bacc.Bacc("TRN2", target_bir_lowering=False, num_devices=1)
    aps = [nc.dram_tensor(k, v.shape, mybir.dt.from_np(v.dtype), kind="ExternalInput").ap() for k, v in arrays.items()]
    out = nc.dram_tensor("out", (NTOK, D), F32, kind="ExternalOutput").ap()
    build(nc, *aps, out)
    r = run_bass_kernel_spmd(nc, [arrays], core_ids=[0])
    return r.results[0]["out"].reshape(B, S, D)
```

```python
from contextlib import ExitStack

import concourse.bass as bass
from concourse import mybir

P = 128
D = 128
S = 64
B = 64
H = 16
DK = D // H
NB = P // S
U = B // NB
G = 2
HG = H // G
HP = H // 2
E = 7
NE = E + 1
I = 352
NTOK = B * S
CH = 3
LAST = I - (CH - 1) * P
SLOTS = (NTOK + E * (P - 1)) // P
ROW = 2 * D + 2
WT, TOK = 2 * D, 2 * D + 1
VW = 2 * NB * (DK + 1)
VALL = 384
NOWHERE = 1.0e6
EPS = 1e-5
KNEE = 8.0
Q_KNEE = 1.0 + 2.718281828459045 ** -KNEE
F32 = mybir.dt.float32
I32 = mybir.dt.int32
ALU = mybir.AluOpType
ACT = mybir.ActivationFunctionType
AX = mybir.AxisListType


def build(nc, x, ctxk, ctxv, wv, bv, wo, bo, rw, rb, wup, wdn, ident, hmask, tri, small, tokens, out):
    ctx = ExitStack()
    with ctx:
        def sb(name, shape, dt=F32):
            return ctx.enter_context(nc.sbuf_tensor(name, shape, dt))

        sems = {}

        def sem(name):
            if name not in sems:
                sems[name] = ctx.enter_context(nc.semaphore(name))
            return sems[name]

        early = sb("early", [P, 3 * U * D])
        x_all = early[:, 0:U * D].rearrange("p (u d) -> p u d", u=U)
        ck_all = early[:, U * D:2 * U * D].rearrange("p (u d) -> p u d", u=U)
        cv_all = early[:, 2 * U * D:3 * U * D].rearrange("p (u d) -> p u d", u=U)
        hs_all = early[:, 0:SLOTS * ROW].rearrange("p (s c) -> p s c", s=SLOTS)
        h_all = sb("h_all", [P, U, D])
        hT_all = sb("hT_all", [P, U, D])
        wup_sb = sb("wup_sb", [P, NE, 2 * I])
        wdn_sb = sb("wdn_sb", [P, NE, CH, D])
        wv_sb = sb("wv_sb", [P, D])
        wo_sb = sb("wo_sb", [P, D])
        rw_sb = sb("rw_sb", [P, E])
        bv_sb = sb("bv_sb", [P, D])
        bo_sb = sb("bo_sb", [P, D])
        rb_sb = sb("rb_sb", [P, E])
        id_sb = sb("id_sb", [P, P])
        hmask_sb = sb("hmask_sb", [P, HG + 2])
        tri_sb = sb("tri_sb", [P, 2, P])
        small_sb = sb("small_sb", [P, U + SLOTS + E])
        thr = small_sb[:, 0:U]
        slot_no = small_sb[:, U:U + SLOTS]
        first_wins = small_sb[:, U + SLOTS:]
        tok_sb = sb("tok_sb", [P, U])
        nowhere_row = sb("nowhere_row", [P, ROW])
        mhalf = sb("mhalf", [P, 1])

        st = {k: sb(f"st_{k}", [P, 6]) for k in "psx"}
        mv = {k: sb(f"mv_{k}", [P, 2]) for k in "psx"}
        ve = {k: sb(f"ve_{k}", [P, 1]) for k in "psx"}
        rs = {k: sb(f"rs_{k}", [P, 1]) for k in "psx"}
        xn = {k: sb(f"xn_{k}", [P, D]) for k in "psx"}
        xnT = sb("xnT", [P, D])
        pn = sb("pn", [P, D])
        pT = sb("pT", [P, G, S])
        q_bd = {"s": [sb(f"q_bd_s{i}", [P, G, P]) for i in range(2)], "x": [sb("q_bd_x", [P, G, P])] * 2}
        k_hd = {k: [sb(f"k_hd_{k}{i}", [P, G, HG, S]) for i in range(2)] for k in "sx"}
        v_bd = {k: [sb(f"v_bd_{k}{i}", [P, VALL]) for i in range(2)] for k in "sx"}
        mx = {k: sb(f"mx_{k}", [P, G, HG]) for k in "sx"}
        pr = {k: sb(f"pr_{k}", [P, G, HG, S]) for k in "sx"}
        prT = {k: sb(f"prT_{k}", [P, G, 4, P]) for k in "sx"}
        rden = {k: sb(f"rden_{k}", [P, HP, 2]) for k in "sx"}
        on = {k: sb(f"on_{k}", [P, HP, 2, DK]) for k in "sx"}
        orow = [sb(f"orow{i}", [P, D]) for i in range(2)]
        onT = sb("onT", [P, D])
        hT = sb("hT", [P, D])

        bank = [ctx.enter_context(nc.psum_tensor(f"bank{i}", [P, 512], F32)) for i in range(8)]
        ps_s = {"s": [bank[0], bank[1]], "x": [bank[2], bank[3]]}
        ps_o = {"s": bank[4], "x": bank[5]}
        ps_xT = ps_p = ps_pT = bank[6][:, 0:P]
        ps_r = bank[6][:, 512 - U * E:].rearrange("p (u e) -> p u e", e=E)
        ps_qT = ps_oT = ps_wo = ps_hT = bank[7][:, 0:P]

        rowb = [sb(f"rowb{i}", [P, ROW]) for i in range(2)]
        place = [sb(f"place{i}", [P, 1], I32) for i in range(2)]
        token = [sb(f"token{i}", [P, 1], I32) for i in range(2)]
        yrow = [sb(f"yrow{i}", [P, D]) for i in range(2)]
        fx = [sb(f"fx{i}", [P, D]) for i in range(2)]
        fhT = [sb(f"fhT{i}", [P, D]) for i in range(2)]
        gate = [sb(f"gate{i}", [P, I]) for i in range(2)]
        gT = [sb(f"gT{i}", [P, CH, P]) for i in range(2)]
        ps_gate = [bank[0], bank[1]]
        ps_up = [bank[2], bank[3]]
        ps_gT = [bank[4], bank[5]]
        ps_y = [bank[6][:, 0:D], bank[7][:, 0:D]]
        ps_fhT = [bank[4][:, CH * P:], bank[5][:, CH * P:]]
        rt = {n: sb(f"rt_{n}", [P, U, E]) for n in ("l", "cl", "q", "pr", "t", "ml", "key", "eq", "oh")}
        r1 = {n: sb(f"r1_{n}", [P, U]) for n in ("max", "win", "p", "tw", "rtw", "c1", "pos")}
        meta = sb("meta", [P, U, 2])
        et = {n: sb(f"et_{n}", [P, E, U]) for n in ("zero", "incl", "pos", "cmp")}
        e1 = {n: sb(f"e1_{n}", [P, E]) for n in ("n", "tiles", "ctiles", "excl", "shift")}
        se_cmp = sb("se_cmp", [P, SLOTS, E])
        se_f = sb("se_f", [P, SLOTS])
        slot_expert = sb("slot_expert", [P, SLOTS], I32)
        ps_pre, ps_tot = bank[7][:, 0:E * U], bank[7][:, E * U:2 * E * U]

        load = lambda eng, dst, src, name: eng.dma_start(dst, src).then_inc(sem(name), 16)

        def at(unit):
            return unit + 1

        def steps(eng, body, n, head, tail):
            for t in range(head):
                body(t, t % 2)
            with eng.Fori(0, (n - head - tail) // 2) as i:
                for k in range(2):
                    body(i * 2 + (head + k), (head + k) % 2)
            for t in range(n - tail, n):
                body(t, t % 2)

        DELAY = {"n": 0, "p": 1, "s": 2, "o": 3, "w": 4, "x": 5, "y": 6, "r": 7}
        A_STEPS, A_PEEL, A_LOOP_END = U + 7, 8, U

        def phase_a(eng, body):
            def one(pair, par, fixed):
                u = {k: pair * 2 + (par - d) for k, d in DELAY.items()}
                parity = {k: (par - d) % 2 for k, d in DELAY.items()}
                u.update({f"{k} pair": pair + (par - d) // 2 for k, d in DELAY.items()})
                body(u, parity, lambda k: not fixed or 0 <= u[k] < U)

            for t in range(A_PEEL):
                one(t // 2, t % 2, True)
            with eng.Fori(A_PEEL // 2, A_LOOP_END // 2) as pair:
                for par in range(2):
                    one(pair, par, False)
            for t in range(A_LOOP_END, A_STEPS):
                one(t // 2, t % 2, True)

        def wait_apart(eng, *waits):
            waits = [(name, value if isinstance(value, int) else eng.snap(eng.to_reg(value))) for name, value in waits]
            eng.wait_ge(sem("ready"), 1)
            for name, value in waits:
                eng.wait_ge(sem(name), value)

        def early_unit(u):
            return isinstance(u, int) and u < 2

        def first_unit(u):
            return isinstance(u, int) and u < 1

        block = ctx.enter_context(nc.Block())

        o_dram = nc.dram_tensor("attention_out", (U, NB, H, S, DK), F32, kind="Internal").ap()
        o_rows = o_dram.rearrange("u b h q d -> (u b h q d)").rearrange("(u p c) -> u p c", p=P, c=D)
        hs_dram = nc.dram_tensor("sorted_rows", (SLOTS * P, ROW), F32, kind="Internal").ap()
        hs_tiles = hs_dram.rearrange("(s p) c -> p s c", p=P)

        @block.sync
        def _(sp):
            xv = x.rearrange("(u p) d -> p u d", p=P)
            load(sp, x_all[:, 0:2, :], xv[:, 0:2, :], "l_x0")
            load(sp, id_sb[:], ident, "l_first")
            load(sp, wv_sb[:], wv, "l_first")
            load(sp, bv_sb[:], bv.partition_broadcast(P), "l_first")
            load(sp, hmask_sb[:], hmask, "l_first")
            load(sp, bo_sb[:], bo.partition_broadcast(P), "l_first")
            load(sp, x_all[:, 2:8, :], xv[:, 2:8, :], "l_x1")
            load(sp, wo_sb[:], wo, "l_second")
            load(sp, rw_sb[:], rw, "l_second")
            load(sp, x_all[:, 8:U, :], xv[:, 8:U, :], "l_x2")

            def body(u, par, live):
                if isinstance(u["n"], int) and u["n"] < 2:
                    load(sp, [ck_all, cv_all][u["n"]][:], [ctxk, ctxv][u["n"]], "l_ctx")
                if isinstance(u["n"], int) and u["n"] == 2:
                    load(sp, rb_sb[:], rb.partition_broadcast(P), "l_router")
                    load(sp, small_sb[:], small.partition_broadcast(P), "l_router")
                    load(sp, tok_sb[:], tokens, "l_router")
                    load(sp, tri_sb[:], tri, "l_router")
                if isinstance(u["n"], int) and 4 <= u["n"] < 8:
                    c = u["n"] - 4
                    if c == CH:
                        load(sp, wup_sb[:], wup, "l_w")
                    else:
                        rows = P if c < CH - 1 else LAST
                        load(sp, wdn_sb[0:rows, :, c, :],
                             wdn[:, c * P:c * P + rows, :].rearrange("e i c -> i e c"), "l_w")
                if live("s"):
                    sp.wait_ge(sem("s_on"), at(u["s"]))
                    for b in range(NB):
                        load(sp, o_dram[u["s"], b, :, :, :].rearrange("h q d -> q h d"),
                             on["s"][S * b:S * (b + 1), :, :, :].rearrange("p a c d -> p (a c) d"), "s_out")
                    wait_apart(sp, ("s_out", 16 * NB * at(u["s"])),
                               *([] if early_unit(u["s"]) else [("s_oT", at(u["s"]) - 2)]))
                    load(sp, orow[par["s"]][:], o_rows[u["s"], :, :], f"w_rows{par['s']}")

                if live("s"):
                    load(sp, hs_tiles[:, u["s"], :], nowhere_row[:, :], "prefilled")

            sp.wait_ge(sem("nowhere"), 1)
            load(sp, hs_tiles[:, U:SLOTS, :],
                 nowhere_row[:, :].unsqueeze(1).broadcast_to([P, SLOTS - U, ROW]), "prefilled")
            phase_a(sp, body)

            for n in range(2):
                sp.wait_ge(sem(f"b_sent{n}"), 16 * (U // 2))
            load(sp, hs_all[:, 0, :], hs_tiles[:, 0, :], "c_row0")
            load(sp, hs_all[:, 1, :], hs_tiles[:, 1, :], "c_row1")
            with sp.Fori(0, (SLOTS - 2) // 2) as i:
                for k in range(2):
                    sp.wait_ge(sem(f"c_row{k}"), i * 16 + 16)
                    load(sp, hs_all[:, i * 2 + (2 + k), :], hs_tiles[:, i * 2 + (2 + k), :], f"c_row{k}")

        N_FIRST, N_SECOND, N_ROUTER = 16 * 5, 16 * 2, 16 * 4

        ones_in_v = lambda v, h2: v[S * h2:S * (h2 + 1), 0:HP * VW].rearrange(
            "p (a b c d) -> p a b c d", a=HP, b=NB, c=2)[:, :, :, h2, DK:DK + 1]

        def v_slots(v, h2):
            return v[S * h2:S * (h2 + 1), 0:HP * VW].rearrange(
                "p (a b c d) -> p a b c d", a=HP, b=NB, c=2)[:, :, :, h2, 0:DK]

        @block.gpsimd
        def _(pool):
            nc.gpsimd.memset(nowhere_row[:, 0:TOK], 0.0)
            nc.gpsimd.memset(nowhere_row[:, TOK:ROW], NOWHERE).then_inc(sem("nowhere"), 1)
            nc.gpsimd.memset(mhalf[:], -0.5).then_inc(sem("ready"), 1)
            for i in range(2):
                nc.gpsimd.memset(q_bd["s"][i][:], 0.0)
            nc.gpsimd.memset(q_bd["x"][0][:], 0.0).then_inc(sem("zeros"), 1)
            for k in "sx":
                for i in range(2):
                    nc.gpsimd.memset(v_bd[k][i][:], 0.0).then_inc(sem("v_zero"), 1)
            pool.wait_ge(sem("v_zero"), 4)
            for k in "sx":
                for i in range(2):
                    for h2 in range(2):
                        nc.gpsimd.memset(ones_in_v(v_bd[k][i], h2), 1.0).then_inc(sem("v_ones"), 1)
            pool.wait_ge(sem("v_ones"), 8)
            pool.wait_ge(sem("ready"), 1)
            pool.wait_ge(sem("l_first"), N_FIRST)

            def rstd(k, u):
                pool.wait_ge(sem(f"{k}_ve"), at(u))
                nc.gpsimd.tensor_tensor(rs[k][:], ve[k][:], mhalf[:], ALU.pow).then_inc(sem(f"{k}_rs"), 1)

            def by_head(k, par, src, u):
                if not early_unit(u):
                    pool.wait_ge(sem(f"{k}_sc"), at(u) * 2 - 4)
                nc.gpsimd.tensor_tensor(
                    k_hd[k][par][:], src.unsqueeze(2).broadcast_to([P, G, HG, S]),
                    hmask_sb[:, 0:HG].unsqueeze(1).unsqueeze(3).broadcast_to([P, G, HG, S]),
                    ALU.mult).then_inc(sem(f"{k}_khd"), 1)

            def body(u, par, live):
                if live("r"):
                    rstd("x", u["r"])
                if live("x"):
                    if first_unit(u["x"]):
                        pool.wait_ge(sem("l_ctx"), 32)
                    by_head("x", par["x"], ck_all[:, u["x"], :].rearrange("p (g k) -> p g k", g=G), u["x"])
                    if not early_unit(u["x"]):
                        wait_apart(pool, ("x_pv", at(u["x"]) * 2 - 4))
                    nc.gpsimd.tensor_tensor(
                        v_bd["x"][par["x"]][:, 0:HP * VW].rearrange("p (a c d) -> p a c d", c=2, d=DK + 1)[:, :, :, 0:DK],
                        cv_all[:, u["x"], :].rearrange("p (a d) -> p a d", d=DK).unsqueeze(2).broadcast_to([P, HP * NB, 2, DK]),
                        hmask_sb[:, HG:HG + 2].unsqueeze(1).unsqueeze(3).broadcast_to([P, HP * NB, 2, DK]),
                        ALU.mult).then_inc(sem("x_v"), 1)
                if live("n"):
                    rstd("p", u["n"])
                if live("w"):
                    rstd("s", u["w"])
                if live("p"):
                    pool.wait_ge(sem("p_xn"), at(u["p"]))
                    nc.gpsimd.tensor_tensor(x_all[:, u["p"], :], x_all[:, u["p"], :], bo_sb[:], ALU.add).then_inc(sem("p_xb"), 1)
                    pool.wait_ge(sem("p_pT"), at(u["p"]))
                    by_head("s", par["p"], pT[:, :, :], u["p"])
                if live("r"):
                    wait_apart(pool, ("x_xn", at(u["r"])))
                    nc.gpsimd.tensor_copy(h_all[:, u["r"], :], xn["x"][:]).then_inc(sem("x_h"), 1)

            phase_a(pool, body)

            pool.wait_ge(sem("prefilled"), 16 * (U + 1))

            def send(n, p):
                wait_apart(pool, ("f_y", at(n)))
                pool.indirect_dma_start(
                    out=hs_dram, out_offset=bass.IndirectOffsetOnAxis(ap=place[p][:, 0:1], axis=0),
                    in_=rowb[p][:, :], in_offset=None).then_inc(sem(f"b_sent{p}"), 16)

            steps(pool, send, U, 0, 0)

            def put(s, p):
                wait_apart(pool, ("f_y", at(s + U)))
                pool.indirect_dma_start(
                    out=out, out_offset=bass.IndirectOffsetOnAxis(ap=token[p][:, 0:1], axis=0),
                    in_=yrow[p][:, :], in_offset=None,
                    bounds_check=NTOK - 1, oob_is_err=False).then_inc(sem(f"c_put{p}"), 16)

            steps(pool, put, SLOTS, 0, 0)
            for n in range(2):
                pool.wait_ge(sem(f"c_put{n}"), 16 * (SLOTS // 2))

        @block.tensor
        def _(pe):
            pe.wait_ge(sem("l_first"), N_FIRST)
            pe.wait_ge(sem("zeros"), 1)
            pe.wait_ge(sem("v_ones"), 8)

            def scores(k, par, u, g):
                if g == 0:
                    pe.wait_ge(sem(f"{k}_khd"), at(u))
                    pe.wait_ge(sem(f"{k}_qbd"), at(u))
                if not first_unit(u):
                    pe.wait_ge(sem(f"{k}_prT{g}"), at(u) - 1)
                nc.tensor.matmul(ps_s[k][g][:, :], q_bd[k][par][:, g, :],
                                 k_hd[k][par][:, g, :, :].rearrange("p h k -> p (h k)"),
                                 start=True, stop=True).then_inc(sem(f"{k}_sc"), 1)

            def turn(k, u, g):
                pe.wait_ge(sem(f"{k}_exp{g}"), at(u))
                for i in range(4):
                    last = nc.tensor.transpose(ps_s[k][g][:, i * P:(i + 1) * P],
                                               pr[k][:, g, 2 * i:2 * i + 2, :].rearrange("p h k -> p (h k)"), id_sb[:])
                last.then_inc(sem(f"{k}_turn{g}"), 1)

            def weigh(k, par, u, g):
                pe.wait_ge(sem(f"{k}_prT{g}"), at(u))
                if g == 0:
                    pe.wait_ge(sem(f"{k}_v"), at(u))
                    if not first_unit(u):
                        pe.wait_ge(sem(f"{k}_on"), at(u) - 1)
                for i in range(4):
                    at_col = (4 * g + i) * VW
                    last = nc.tensor.matmul(ps_o[k][:, at_col:at_col + P], prT[k][:, g, i, :],
                                            v_bd[k][par][:, at_col:at_col + P], start=True, stop=True)
                last.then_inc(sem(f"{k}_pv"), 1)

            def reached(u, ahead):
                return min(at(u) + ahead, U) if isinstance(u, int) else at(u) + ahead

            def body(u, par, live):
                if live("p"):
                    pe.wait_ge(sem("p_xn"), at(u["p"]))
                    if not first_unit(u["p"]):
                        pe.wait_ge(sem("s_qbd"), at(u["p"]) - 1)
                    nc.tensor.transpose(ps_xT, xn["p"][:], id_sb[:]).then_inc(sem("p_xT"), 1)
                if live("x"):
                    pe.wait_ge(sem("s_xn"), at(u["x"]))
                    if not (isinstance(u["x"], int) and u["x"] < 3):
                        pe.wait_ge(sem("r_hTall"), at(u["x"]) - 3)
                    nc.tensor.transpose(ps_qT, xn["s"][:], id_sb[:]).then_inc(sem("s_qT"), 1)
                if live("s"):
                    scores("s", par["s"], u["s"], 0)
                if live("y"):
                    turn("x", u["y"], 0)
                if live("w"):
                    if first_unit(u["w"]):
                        pe.wait_ge(sem("l_second"), N_SECOND)
                    pe.wait_ge(sem(f"w_rows{par['w']}"), at(u["w pair"]) * 16)
                    if not first_unit(u["w"]):
                        pe.wait_ge(sem("x_qbd"), at(u["w"]) - 1)
                    nc.tensor.transpose(ps_oT, orow[par["w"]][:], id_sb[:]).then_inc(sem("s_oT"), 1)
                if live("s"):
                    scores("s", par["s"], u["s"], 1)
                if live("y"):
                    turn("x", u["y"], 1)
                if live("p"):
                    pe.wait_ge(sem("p_xnT"), at(u["p"]))
                    nc.tensor.matmul(ps_p, xnT[:], wv_sb[:], start=True, stop=True).then_inc(sem("p_p"), 1)
                if live("w"):
                    pe.wait_ge(sem("s_onT"), at(u["w"]))
                    nc.tensor.matmul(ps_wo, onT[:], wo_sb[:], start=True, stop=True).then_inc(sem("s_wo"), 1)
                if live("y"):
                    weigh("x", par["y"], u["y"], 0)
                    weigh("x", par["y"], u["y"], 1)
                if live("x"):
                    scores("x", par["x"], u["x"], 0)
                if live("s"):
                    turn("s", u["s"], 0)
                if live("p"):
                    pe.wait_ge(sem("p_pn"), at(u["p"]))
                    nc.tensor.transpose(ps_pT, pn[:], id_sb[:]).then_inc(sem("p_T"), 1)
                if live("x"):
                    scores("x", par["x"], u["x"], 1)
                if live("s"):
                    turn("s", u["s"], 1)
                if live("r"):
                    pe.wait_ge(sem("x_xn"), at(u["r"]))
                    pe.wait_ge(sem("s_x"), reached(u["r"], 3))
                    pe.wait_ge(sem("x_qbd"), reached(u["r"], 2))
                    if not live("x"):
                        pe.wait_ge(sem("r_hTall"), at(u["r"]) - 1)
                    nc.tensor.transpose(ps_hT, xn["x"][:], id_sb[:]).then_inc(sem("r_hT"), 1)
                if live("s"):
                    weigh("s", par["s"], u["s"], 0)
                    weigh("s", par["s"], u["s"], 1)
                if live("r"):
                    pe.wait_ge(sem("r_hTs"), at(u["r"]))
                    pe.wait_ge(sem("s_qbd"), reached(u["r"], 6))
                    nc.tensor.matmul(ps_r[:, u["r"], :], hT[:], rw_sb[:], start=True, stop=True).then_inc(sem("r_r"), 1)

            phase_a(pe, body)

            pe.wait_ge(sem("l_w"), 16 * (1 + CH))

            def up(n, p, expert, turned_in=False):
                if not turned_in:
                    pe.wait_ge(sem("f_hT"), at(n))
                nc.tensor.matmul(ps_gate[p][:, 0:I], fhT[p][:], wup_sb[:, expert, 0:I],
                                 start=True, stop=True).then_inc(sem("f_gate"), 1)
                nc.tensor.matmul(ps_up[p][:, 0:I], fhT[p][:], wup_sb[:, expert, I:2 * I],
                                 start=True, stop=True).then_inc(sem("f_up"), 1)

            def turn_g(n, p):
                pe.wait_ge(sem("f_g"), at(n))
                for c in range(CH):
                    w = P if c < CH - 1 else LAST
                    last = nc.tensor.transpose(ps_gT[p][0:w, c * P:(c + 1) * P], gate[p][:, c * P:c * P + w], id_sb[:])
                last.then_inc(sem("f_turn"), 1)

            def down(n, p, expert):
                pe.wait_ge(sem("f_gT"), at(n))
                if not early_unit(n):
                    pe.wait_ge(sem("f_y"), at(n) - 2)
                for c in range(CH):
                    w = P if c < CH - 1 else LAST
                    last = nc.tensor.matmul(ps_y[p], gT[p][0:w, c, :], wdn_sb[0:w, expert, c, :],
                                            start=(c == 0), stop=(c == CH - 1))
                last.then_inc(sem("f_down"), 1)

            def shared(n, p):
                if isinstance(n, int) and n == 2:
                    pe.wait_ge(sem("placed"), 1)
                if not first_unit(n):
                    down(n - 1, 1 - p, E)
                turn_g(n, p)
                if not (isinstance(n, int) and n + 2 >= U):
                    up(n + 2, p, E)

            up(0, 0, E)
            up(1, 1, E)
            pe.wait_ge(sem("l_router"), N_ROUTER)
            pe.wait_ge(sem("chosen"), 1)
            by_et = rt["oh"][:].rearrange("p u e -> p e u")
            nc.tensor.matmul(ps_pre, tri_sb[:, 0, :], by_et, start=True, stop=True)
            nc.tensor.matmul(ps_tot, tri_sb[:, 1, :], by_et, start=True, stop=True).then_inc(sem("counted"), 1)
            steps(pe, shared, U, 4, 2)
            down(U - 1, (U - 1) % 2, E)

            def experts(first, number):
                where = slice(first, first + number) if isinstance(first, int) else bass.ds(first, number)
                return nc.values_load_multi_w_load_instructions(
                    slot_expert[0:1, where], engines=[mybir.EngineType.PE], min_val=0, max_val=E - 1,
                    skip_runtime_bounds_check_because="a count of 0/1 comparisons, clamped to E - 1 by DVE")[1]

            def expert_of(s):
                return experts(s, 1)[0]

            def experts_of(s):
                if isinstance(s, int) and (s < 1 or s + 2 >= SLOTS):
                    return (None if s < 1 else expert_of(s - 1), None if s + 2 >= SLOTS else expert_of(s + 2))
                four = experts(s - 1, 4)
                return four[0], four[3]

            def to_hT(s, p):
                pe.wait_ge(sem("c_fx"), at(s))
                nc.tensor.transpose(ps_fhT[p], fx[p][:], id_sb[:]).then_inc(sem("c_hT"), 1)

            def routed(s, p):
                tail = isinstance(s, int)
                before, ahead = experts_of(s)
                if not first_unit(s):
                    down(s + (U - 1), 1 - p, before)
                if not (tail and s + 3 >= SLOTS):
                    to_hT(s + 3, 1 - p)
                pe.wait_ge(sem("f_hT"), min(at(s + U) + 2, U + SLOTS) if tail else at(s + U) + 2)
                turn_g(s + U, p)
                if not (tail and s + 2 >= SLOTS):
                    up(s + (U + 2), p, ahead, turned_in=True)

            pe.wait_ge(sem("f_gT"), U)
            to_hT(0, 0)
            to_hT(1, 1)
            up(U, 0, expert_of(0))
            up(U + 1, 1, expert_of(1))
            to_hT(2, 0)
            steps(pe, routed, SLOTS, 2, 4)
            down(U + SLOTS - 1, (SLOTS - 1) % 2, expert_of(SLOTS - 1))

        @block.scalar
        def _(act):
            act.wait_ge(sem("zeros"), 1)

            def block_diagonal(k, par, u, src, wait):
                act.wait_ge(sem(wait), at(u))
                if k == "s":
                    if not early_unit(u):
                        act.wait_ge(sem("s_sc"), at(u) * 2 - 4)
                elif not first_unit(u):
                    act.wait_ge(sem("x_sc"), at(u) * 2 - 2)
                for g in range(G):
                    for b in range(NB):
                        last = nc.scalar.copy(q_bd[k][par][S * b:S * (b + 1), g, S * b:S * (b + 1)],
                                              src[S * g:S * (g + 1), S * b:S * (b + 1)])
                last.then_inc(sem(f"{k}_qbd"), 1)

            def exp(k, u, g):
                act.wait_ge(sem(f"{k}_sub{g}"), at(u))
                nc.scalar.activation(pr[k][:, g, :, :], pr[k][:, g, :, :], ACT.Exp,
                                     scale=float(DK) ** -0.5).then_inc(sem(f"{k}_exp{g}"), 1)

            def turned(k, u, g):
                act.wait_ge(sem(f"{k}_turn{g}"), at(u))
                if not first_unit(u):
                    act.wait_ge(sem(f"{k}_pv"), 2 * at(u) - 3 + g)
                nc.scalar.copy(prT[k][:, g, :, :].rearrange("p i q -> p (i q)"), ps_s[k][g][:, :]).then_inc(sem(f"{k}_prT{g}"), 1)

            def body(u, par, live):
                if live("p"):
                    act.wait_ge(sem("p_xT"), at(u["p"]))
                    nc.scalar.copy(xnT[:], ps_xT).then_inc(sem("p_xnT"), 1)
                if live("x"):
                    block_diagonal("x", par["x"], u["x"], ps_qT, "s_qT")
                if live("w"):
                    act.wait_ge(sem("s_oT"), at(u["w"]))
                    nc.scalar.copy(onT[:], ps_oT).then_inc(sem("s_onT"), 1)
                if live("y"):
                    turned("x", u["y"], 0)
                    turned("x", u["y"], 1)
                if live("s"):
                    exp("s", u["s"], 0)
                    exp("s", u["s"], 1)
                if live("p"):
                    act.wait_ge(sem("p_pn"), at(u["p"]))
                    if not early_unit(u["p"]):
                        act.wait_ge(sem("s_pv"), at(u["p"]) * 2 - 4)
                    for b in range(NB):
                        for h2 in range(2):
                            src = pn[S * b:S * (b + 1), :].rearrange("p (a c d) -> p a c d", a=HP, c=2)[:, :, h2, :]
                            last = nc.scalar.copy(v_slots(v_bd["s"][par["p"]], h2)[:, :, b, :], src)
                    last.then_inc(sem("s_v"), 1)
                    act.wait_ge(sem("p_T"), at(u["p"]))
                    if not first_unit(u["p"]):
                        act.wait_ge(sem("s_khd"), at(u["p"]) - 1)
                    for g in range(G):
                        for b in range(NB):
                            last = nc.scalar.copy(pT[S * b:S * (b + 1), g, :], ps_pT[S * g:S * (g + 1), S * b:S * (b + 1)])
                    last.then_inc(sem("p_pT"), 1)
                if live("s"):
                    turned("s", u["s"], 0)
                if live("p"):
                    block_diagonal("s", par["p"], u["p"], ps_pT, "p_T")
                if live("s"):
                    turned("s", u["s"], 1)
                if live("r"):
                    act.wait_ge(sem("r_hT"), at(u["r"]))
                    if not first_unit(u["r"]):
                        act.wait_ge(sem("r_r"), at(u["r"]) - 1)
                    nc.scalar.copy(hT[:], ps_hT).then_inc(sem("r_hTs"), 1)
                    nc.scalar.copy(hT_all[:, u["r"], :], ps_hT).then_inc(sem("r_hTall"), 1)
                if live("x"):
                    exp("x", u["x"], 0)
                    exp("x", u["x"], 1)

            phase_a(act, body)

            def silu(n, p):
                act.wait_ge(sem("f_gate"), at(n))
                if not early_unit(n):
                    act.wait_ge(sem("f_turn"), at(n) - 2)
                nc.scalar.activation(gate[p][:], ps_gate[p][:, 0:I], ACT.Silu).then_inc(sem("f_act"), 1)

            def gate_turned(n, p):
                act.wait_ge(sem("f_turn"), at(n))
                if not early_unit(n):
                    act.wait_ge(sem("f_down"), at(n) - 2)
                nc.scalar.copy(gT[p][:, 0:CH - 1, :].rearrange("p c q -> p (c q)"), ps_gT[p][:, 0:(CH - 1) * P])
                nc.scalar.copy(gT[p][0:LAST, CH - 1, :], ps_gT[p][0:LAST, (CH - 1) * P:CH * P]).then_inc(sem("f_gT"), 1)

            def copy_hT(n, p):
                if not early_unit(n):
                    act.wait_ge(sem("f_up"), at(n) - 2)
                nc.scalar.copy(fhT[p][:], hT_all[:, n, :]).then_inc(sem("f_hT"), 1)

            def shared(n, p):
                if not (isinstance(n, int) and n + 1 >= U):
                    silu(n + 1, 1 - p)
                if not (isinstance(n, int) and n + 3 >= U):
                    copy_hT(n + 3, 1 - p)
                gate_turned(n, p)

            act.wait_ge(sem("r_hTall"), U)
            copy_hT(0, 0)
            copy_hT(1, 1)
            act.wait_ge(sem("clipped"), 1)
            nc.scalar.activation(rt["q"][:], rt["cl"][:], ACT.Exp, scale=-1.0).then_inc(sem("exped"), 1)
            silu(0, 0)
            copy_hT(2, 0)
            steps(act, shared, U, 3, 3)

            def routed_hT(s, p):
                act.wait_ge(sem("c_hT"), at(s))
                act.wait_ge(sem("f_up"), at(s + U) - 2)
                nc.scalar.copy(fhT[p][:], ps_fhT[p]).then_inc(sem("f_hT"), 1)

            def routed(s, p):
                if not (isinstance(s, int) and s + 1 >= SLOTS):
                    silu(s + (U + 1), 1 - p)
                if not (isinstance(s, int) and s + 3 >= SLOTS):
                    routed_hT(s + 3, 1 - p)
                gate_turned(s + U, p)

            routed_hT(0, 0)
            routed_hT(1, 1)
            silu(U, 0)
            routed_hT(2, 0)
            steps(act, routed, SLOTS, 3, 3)

        @block.vector
        def _(dve):
            done = [0]

            def link(ins):
                done[0] += 1
                ins.then_inc(sem("chain"), 1)
                dve.wait_ge(sem("chain"), done[0])

            def moments(k, src, u):
                nc.vector.bn_stats(st[k][:], src).then_inc(sem(f"{k}_st"), 1)

            def mean_variance(k, u):
                wait_apart(dve, (f"{k}_st", at(u)))
                nc.vector.bn_aggr(mv[k][:], st[k][:]).then_inc(sem(f"{k}_mv"), 1)

            def variance_eps(k, u):
                dve.wait_ge(sem(f"{k}_mv"), at(u))
                nc.vector.tensor_scalar(ve[k][:], mv[k][:, 1:2], EPS, None, ALU.add).then_inc(sem(f"{k}_ve"), 1)

            def normed(k, src, u):
                dve.wait_ge(sem(f"{k}_rs"), at(u))
                nc.vector.tensor_scalar(xn[k][:], src, mv[k][:, 0:1], rs[k][:, 0:1], ALU.subtract, ALU.mult).then_inc(sem(f"{k}_xn"), 1)

            def scores_of(k, g):
                return ps_s[k][g][:, :].rearrange("p (h k) -> p h k", h=HG)

            def maximum(k, u, g):
                dve.wait_ge(sem(f"{k}_sc"), 2 * at(u) - 1 + g)
                nc.vector.tensor_reduce(mx[k][:, g, :], scores_of(k, g), AX.X, ALU.max).then_inc(sem(f"{k}_mx"), 1)

            def soften(k, u, g):
                dve.wait_ge(sem(f"{k}_mx"), 2 * at(u) - 1 + g)
                if not first_unit(u):
                    dve.wait_ge(sem(f"{k}_turn{g}"), at(u) - 1)
                nc.vector.tensor_tensor(pr[k][:, g, :, :], scores_of(k, g), mx[k][:, g, :].unsqueeze(2).broadcast_to([P, HG, S]),
                                        ALU.subtract).then_inc(sem(f"{k}_sub{g}"), 1)

            def sums(k, b):
                return ps_o[k][S * b:S * (b + 1), 0:HP * VW].rearrange("p (a b c d) -> p a b c d", a=HP, b=NB, c=2)[:, :, b, :, :]

            def invert(k, u):
                dve.wait_ge(sem(f"{k}_pv"), 2 * at(u))
                for b in range(NB):
                    last = nc.vector.reciprocal(rden[k][S * b:S * (b + 1), :, :], sums(k, b)[:, :, :, DK])
                last.then_inc(sem(f"{k}_rden"), 1)

            def normalise(k, u):
                dve.wait_ge(sem(f"{k}_rden"), at(u))
                if k == "s" and not first_unit(u):
                    dve.wait_ge(sem("s_out"), 16 * NB * (at(u) - 1))
                for b in range(NB):
                    rows = slice(S * b, S * (b + 1))
                    last = nc.vector.tensor_tensor(on[k][rows, :, :, :], sums(k, b)[:, :, :, 0:DK],
                                                   rden[k][rows, :, :].unsqueeze(3).broadcast_to([S, HP, 2, DK]), ALU.mult)
                last.then_inc(sem(f"{k}_on"), 1)

            def body(u, par, live):
                x_of = lambda k: x_all[:, u[k], :]
                if live("o"):
                    invert("s", u["o"])
                if live("r"):
                    if not first_unit(u["r"]):
                        dve.wait_ge(sem("r_hT"), at(u["r"]) - 1)
                        dve.wait_ge(sem("x_h"), at(u["r"]) - 1)
                    normed("x", x_all[:, u["r"], :], u["r"])
                if live("o"):
                    normalise("s", u["o"])
                if live("s"):
                    maximum("s", u["s"], 0)
                if live("n"):
                    if isinstance(u["n"], int) and u["n"] in X_LOADS:
                        dve.wait_ge(sem(X_LOADS[u["n"]]), 16)
                    moments("p", x_all[:, u["n"], :], u["n"])
                if live("s"):
                    soften("s", u["s"], 0)
                    maximum("s", u["s"], 1)
                if live("p"):
                    dve.wait_ge(sem("p_p"), at(u["p"]))
                    if not first_unit(u["p"]):
                        dve.wait_ge(sem("p_T"), at(u["p"]) - 1)
                        dve.wait_ge(sem("s_v"), at(u["p"]) - 1)
                    nc.vector.tensor_tensor(pn[:], ps_p, bv_sb[:], ALU.add).then_inc(sem("p_pn"), 1)
                if live("s"):
                    soften("s", u["s"], 1)
                if live("n"):
                    mean_variance("p", u["n"])
                if live("w"):
                    dve.wait_ge(sem("p_xb"), at(u["w"]))
                    dve.wait_ge(sem("s_wo"), at(u["w"]))
                    nc.vector.tensor_tensor(x_of("w"), ps_wo, x_of("w"), ALU.add).then_inc(sem("s_x"), 1)
                if live("n"):
                    variance_eps("p", u["n"])
                if live("w"):
                    wait_apart(dve, ("s_x", at(u["w"])))
                    moments("s", x_of("w"), u["w"])
                    mean_variance("s", u["w"])
                if live("y"):
                    invert("x", u["y"])
                if live("w"):
                    variance_eps("s", u["w"])
                if live("n"):
                    if not first_unit(u["n"]):
                        dve.wait_ge(sem("p_xT"), at(u["n"]) - 1)
                    normed("p", x_all[:, u["n"], :], u["n"])
                if live("y"):
                    normalise("x", u["y"])
                if live("x"):
                    maximum("x", u["x"], 0)
                if live("y"):
                    dve.wait_ge(sem("x_on"), at(u["y"]))
                    nc.vector.tensor_tensor(x_of("y"), x_of("y"), on["x"][:].rearrange("p a b d -> p (a b d)"), ALU.add).then_inc(sem("x_x"), 1)
                if live("x"):
                    soften("x", u["x"], 0)
                if live("y"):
                    wait_apart(dve, ("x_x", at(u["y"])))
                    moments("x", x_of("y"), u["y"])
                if live("x"):
                    maximum("x", u["x"], 1)
                if live("y"):
                    mean_variance("x", u["y"])
                if live("w"):
                    if not first_unit(u["w"]):
                        dve.wait_ge(sem("s_qT"), at(u["w"]) - 1)
                    normed("s", x_of("w"), u["w"])
                if live("x"):
                    soften("x", u["x"], 1)
                if live("y"):
                    variance_eps("x", u["y"])

            X_LOADS = {0: "l_x0", 2: "l_x1", A_PEEL - 1: "l_x2"}
            dve.wait_ge(sem("l_first"), N_FIRST)
            phase_a(dve, body)

            def gated(n, p):
                dve.wait_ge(sem("f_act"), at(n))
                dve.wait_ge(sem("f_up"), at(n))
                nc.vector.tensor_tensor(gate[p][:], gate[p][:], ps_up[p][:, 0:I], ALU.mult).then_inc(sem("f_g"), 1)

            def shared_row(n, p, sent):
                if sent is not None:
                    dve.wait_ge(sem(f"b_sent{p}"), sent)
                nc.vector.tensor_copy(rowb[p][:, 0:D], h_all[:, n, :])
                nc.vector.tensor_copy(rowb[p][:, WT:ROW], meta[:, n, :])
                nc.vector.tensor_copy(place[p][:], r1["pos"][:, n:n + 1] if isinstance(n, int) else r1["pos"][:, bass.ds(n, 1)])
                dve.wait_ge(sem("f_down"), at(n))
                nc.vector.scalar_tensor_tensor(
                    rowb[p][:, D:2 * D], ps_y[p], r1["c1"][:, n:n + 1] if isinstance(n, int) else r1["c1"][:, bass.ds(n, 1)],
                    x_all[:, n, :], ALU.mult, ALU.add).then_inc(sem("f_y"), 1)
                dve.wait_ge(sem("f_y"), at(n))

            def b_step(n, p, sent):
                if not (isinstance(n, int) and n + 1 >= U):
                    gated(n + 1, 1 - p)
                if not first_unit(n):
                    shared_row(n - 1, 1 - p, sent)

            bce = lambda a: a.unsqueeze(2).broadcast_to([P, U, E])
            bcu = lambda a: a.unsqueeze(1).broadcast_to([P, U, E])
            dve.wait_ge(sem("r_r"), U)
            dve.wait_ge(sem("l_router"), N_ROUTER)
            link(nc.vector.tensor_tensor(rt["l"][:], ps_r, bcu(rb_sb[:, :]), ALU.add))
            nc.vector.tensor_scalar(rt["cl"][:], rt["l"][:], -50.0, 50.0, ALU.max, ALU.min).then_inc(sem("clipped"), 1)
            dve.wait_ge(sem("exped"), 1)
            link(nc.vector.tensor_scalar(rt["q"][:], rt["q"][:], 1.0, None, ALU.add))
            nc.vector.reciprocal(rt["pr"][:], rt["q"][:])
            nc.vector.tensor_scalar(rt["ml"][:], rt["cl"][:], KNEE, None, ALU.min)
            link(nc.vector.tensor_scalar(rt["t"][:], rt["q"][:], Q_KNEE, Q_KNEE, ALU.min, ALU.subtract))
            link(nc.vector.scalar_tensor_tensor(rt["key"][:], rt["t"][:], -8.0, rt["ml"][:], ALU.mult, ALU.add))
            link(nc.vector.tensor_reduce(r1["max"][:], rt["key"][:], AX.X, ALU.max))
            link(nc.vector.tensor_tensor(rt["eq"][:], rt["key"][:], bce(r1["max"][:, :]), ALU.is_ge))
            link(nc.vector.tensor_tensor(rt["t"][:], rt["eq"][:], bcu(first_wins), ALU.mult))
            link(nc.vector.tensor_reduce(r1["win"][:], rt["t"][:], AX.X, ALU.max))
            nc.vector.tensor_tensor(rt["oh"][:], rt["t"][:], bce(r1["win"][:, :]), ALU.is_equal).then_inc(sem("chosen"), 1)
            dve.wait_ge(sem("chosen"), 1)
            gated(0, 0)
            b_step(0, 0, None)
            link(nc.vector.tensor_tensor(rt["pr"][:], rt["pr"][:], rt["oh"][:], ALU.mult))
            link(nc.vector.tensor_reduce(r1["p"][:], rt["pr"][:], AX.X, ALU.add))
            link(nc.vector.tensor_scalar(r1["p"][:], r1["p"][:], 1e-8, 1.0 - 1e-8, ALU.max, ALU.min))
            link(nc.vector.tensor_scalar(r1["tw"][:], r1["p"][:], 0.5, 1e-8, ALU.add, ALU.add))
            link(nc.vector.tensor_scalar(r1["tw"][:], r1["tw"][:], 0.5, 2.0, ALU.max, ALU.min))
            link(nc.vector.reciprocal(r1["rtw"][:], r1["tw"][:]))
            nc.vector.tensor_scalar(r1["c1"][:], r1["rtw"][:], 0.5, None, ALU.mult)
            link(nc.vector.tensor_tensor(meta[:, :, 0], r1["rtw"][:], r1["p"][:], ALU.mult))
            nc.vector.tensor_copy(meta[:, :, 1], tok_sb[:])
            nc.vector.memset(et["zero"][:], 0.0)
            dve.wait_ge(sem("counted"), 1)
            flat = lambda a: a.rearrange("p e u -> p (e u)")
            tot = ps_tot.rearrange("p (e u) -> p e u", e=E)
            link(nc.vector.tensor_reduce(e1["n"][:], tot, AX.X, ALU.add))
            link(nc.vector.tensor_tensor_scan(flat(et["incl"][:]), ps_tot, flat(et["zero"][:]), 0.0, ALU.add, ALU.add))
            link(nc.vector.tensor_tensor(et["cmp"][:], e1["n"][:, :].unsqueeze(2).broadcast_to([P, E, U]),
                                         thr.unsqueeze(1).broadcast_to([P, E, U]), ALU.is_gt))
            link(nc.vector.tensor_reduce(e1["tiles"][:], et["cmp"][:], AX.X, ALU.add))
            link(nc.vector.tensor_tensor_scan(e1["ctiles"][:], e1["tiles"][:], et["zero"][:, 0, 0:E], 0.0, ALU.add, ALU.add))
            link(nc.vector.tensor_tensor(e1["shift"][:], e1["ctiles"][:], e1["tiles"][:], ALU.subtract))
            link(nc.vector.tensor_tensor(e1["excl"][:], et["incl"][:, :, U - 1], e1["n"][:], ALU.subtract))
            link(nc.vector.scalar_tensor_tensor(e1["shift"][:], e1["shift"][:], float(P), e1["excl"][:], ALU.mult, ALU.subtract))
            link(nc.vector.tensor_tensor(flat(et["pos"][:]), flat(et["incl"][:]), ps_tot, ALU.subtract))
            link(nc.vector.tensor_tensor(flat(et["pos"][:]), flat(et["pos"][:]), ps_pre, ALU.add))
            link(nc.vector.tensor_tensor(et["pos"][:], et["pos"][:], e1["shift"][:, :].unsqueeze(2).broadcast_to([P, E, U]), ALU.add))
            link(nc.vector.tensor_tensor(et["pos"][:], et["pos"][:], rt["oh"][:].rearrange("p u e -> p e u"), ALU.mult))
            link(nc.vector.tensor_reduce(r1["pos"][:], et["pos"][:].rearrange("p e u -> p u e"), AX.X, ALU.add))
            link(nc.vector.tensor_tensor(se_cmp[:], slot_no.unsqueeze(2).broadcast_to([P, SLOTS, E]),
                                         e1["ctiles"][:, :].unsqueeze(1).broadcast_to([P, SLOTS, E]), ALU.is_ge))
            link(nc.vector.tensor_reduce(se_f[:], se_cmp[:], AX.X, ALU.add))
            nc.vector.tensor_scalar(slot_expert[:], se_f[:], float(E - 1), None, ALU.min).then_inc(sem("placed"), 1)

            dve.wait_ge(sem("placed"), 1)
            dve.wait_ge(sem("x_h"), U)
            PEEL = 4
            for n in range(1, PEEL):
                b_step(n, n % 2, 16 * ((n - 1) // 2) if n >= 3 else None)
            with dve.Fori(0, (U - PEEL - 2) // 2) as i:
                for k in range(2):
                    b_step(i * 2 + (PEEL + k), k, i * 16 + 16 * ((PEEL + k - 1) // 2))
            for n in range(U - 2, U):
                b_step(n, n % 2, 16 * ((n - 1) // 2))
            shared_row(U - 1, (U - 1) % 2, 16 * ((U - 1) // 2))

            def routed_in(s, p, landed):
                dve.wait_ge(sem(f"c_row{p}"), landed)
                if not early_unit(s):
                    dve.wait_ge(sem("c_hT"), at(s) - 2)
                nc.vector.tensor_copy(fx[p][:], hs_all[:, s, 0:D]).then_inc(sem("c_fx"), 1)

            def routed_row(s, p, put):
                if put is not None:
                    dve.wait_ge(sem(f"c_put{p}"), put)
                nc.vector.tensor_copy(token[p][:], hs_all[:, s, TOK:ROW])
                dve.wait_ge(sem("f_down"), at(s + U))
                nc.vector.scalar_tensor_tensor(yrow[p][:], ps_y[p], hs_all[:, s, WT:WT + 1], hs_all[:, s, D:2 * D],
                                               ALU.mult, ALU.add).then_inc(sem("f_y"), 1)
                dve.wait_ge(sem("f_y"), at(s + U))

            def c_step(s, p, landed, put):
                if not (isinstance(s, int) and s + 1 >= SLOTS):
                    gated(s + (U + 1), 1 - p)
                if landed is not None:
                    routed_in(s + 4, p, landed)
                if not first_unit(s):
                    routed_row(s - 1, 1 - p, put)

            for s in range(3):
                routed_in(s, s % 2, 16 * (s // 2 + 1))
            gated(U, 0)
            routed_in(3, 1, 32)
            for s in range(PEEL):
                c_step(s, s % 2, 16 * ((s + 4) // 2 + 1), 16 * ((s - 1) // 2) if s >= 3 else None)
            with dve.Fori(0, (SLOTS - 4 - PEEL) // 2) as i:
                for k in range(2):
                    c_step(i * 2 + (PEEL + k), k, i * 16 + 16 * ((PEEL + k + 4) // 2 + 1), i * 16 + 16 * ((PEEL + k - 1) // 2))
            for s in range(SLOTS - 4, SLOTS):
                c_step(s, s % 2, None, 16 * ((s - 1) // 2))
            routed_row(SLOTS - 1, (SLOTS - 1) % 2, 16 * ((SLOTS - 1) // 2))


def kernel(**inputs):
    import numpy as np
    import concourse.bacc as bacc
    from concourse.bass_utils import run_bass_kernel_spmd

    a = {k: np.asarray(v) for k, v in inputs.items()}
    f32 = np.float32
    c = a["ctx_1024"]
    p = np.arange(P)
    arrays = {
        "x": a["x"].reshape(NTOK, D),
        "ctxk": c.reshape(U, NB, S, G, HG * DK).transpose(1, 4, 0, 3, 2).reshape(P, U, D),
        "ctxv": c.reshape(U, NB, S, HP, 2, DK).transpose(4, 2, 0, 3, 1, 5).reshape(P, U, D),
        "wv": a["L0_attn_Wv"].T, "bv": a["L0_attn_bv"], "wo": a["L0_attn_Wo"].T, "bo": a["L0_attn_bo"],
        "rw": a["L0_ffn_router_w"].T, "rb": a["L0_ffn_routing_bias"],
        "wup": np.concatenate([np.concatenate([a["L0_ffn_ew1"], a["L0_ffn_sw1"][None]]),
                               np.concatenate([a["L0_ffn_ew3"], a["L0_ffn_sw3"][None]])], axis=1).transpose(2, 0, 1),
        "wdn": np.concatenate([a["L0_ffn_ew2"], a["L0_ffn_sw2"][None]]).transpose(0, 2, 1),
        "ident": np.eye(P, dtype=f32),
        "hmask": np.concatenate([(p[:, None] // DK) % HG == np.arange(HG)[None],
                                 p[:, None] // S == np.arange(2)[None]], axis=1).astype(f32),
        "tri": np.stack([np.triu(np.ones((P, P), f32), 1), np.ones((P, P), f32)], axis=1),
        "small": np.concatenate([np.arange(U) * P, np.arange(SLOTS), E - np.arange(E)]).astype(f32),
        "tokens": (p[:, None] + P * np.arange(U)[None]).astype(f32),
    }
    arrays = {f"in_{k}": np.ascontiguousarray(v) for k, v in arrays.items()}
    nc = bacc.Bacc("TRN2", target_bir_lowering=False, num_devices=1)
    aps = [nc.dram_tensor(k, v.shape, mybir.dt.from_np(v.dtype), kind="ExternalInput").ap() for k, v in arrays.items()]
    out = nc.dram_tensor("out", (NTOK, D), F32, kind="ExternalOutput").ap()
    build(nc, *aps, out)
    r = run_bass_kernel_spmd(nc, [arrays], core_ids=[0])
    return r.results[0]["out"].reshape(B, S, D)
```

```python
from contextlib import ExitStack

import concourse.bass as bass
from concourse import mybir

P = 128
D = 128
S = 64
B = 64
H = 16
DK = D // H
NB = P // S
U = B // NB
G = 2
HG = H // G
HP = H // 2
E = 7
NE = E + 1
I = 352
NTOK = B * S
CH = 3
LAST = I - (CH - 1) * P
SLOTS = (NTOK + E * (P - 1)) // P
NROW = 4
ROW = 2 * D + 2
WT, TOK = 2 * D, 2 * D + 1
VW = 2 * NB * (DK + 1)
VALL = 384
NOWHERE = 1.0e6
EPS = 1e-5
KNEE = 8.0
Q_KNEE = 1.0 + 2.718281828459045 ** -KNEE
F32 = mybir.dt.float32
I32 = mybir.dt.int32
ALU = mybir.AluOpType
ACT = mybir.ActivationFunctionType
AX = mybir.AxisListType


def build(nc, x, ctxk, ctxv, wv, bv, wo, bo, rw, rb, wup, wdn, ident, hmask, tri, small, tokens, out):
    ctx = ExitStack()
    with ctx:
        def sb(name, shape, dt=F32):
            return ctx.enter_context(nc.sbuf_tensor(name, shape, dt))

        sems = {}

        def sem(name):
            if name not in sems:
                sems[name] = ctx.enter_context(nc.semaphore(name))
            return sems[name]

        early = sb("early", [P, 3 * U * D])
        x_all = early[:, 0:U * D].rearrange("p (u d) -> p u d", u=U)
        ck_all = early[:, U * D:2 * U * D].rearrange("p (u d) -> p u d", u=U)
        cv_all = early[:, 2 * U * D:3 * U * D].rearrange("p (u d) -> p u d", u=U)
        hs_all = early[:, 0:SLOTS * ROW].rearrange("p (s c) -> p s c", s=SLOTS)
        h_all = sb("h_all", [P, U, D])
        hT_all = sb("hT_all", [P, U, D])
        wup_sb = sb("wup_sb", [P, NE, 2 * I])
        wdn_sb = sb("wdn_sb", [P, NE, CH, D])
        wv_sb = sb("wv_sb", [P, D])
        wo_sb = sb("wo_sb", [P, D])
        rw_sb = sb("rw_sb", [P, E])
        bv_sb = sb("bv_sb", [P, D])
        bo_sb = sb("bo_sb", [P, D])
        rb_sb = sb("rb_sb", [P, E])
        id_sb = sb("id_sb", [P, P])
        hmask_sb = sb("hmask_sb", [P, HG + 2])
        tri_sb = sb("tri_sb", [P, 2, P])
        small_sb = sb("small_sb", [P, U + SLOTS + E])
        thr = small_sb[:, 0:U]
        slot_no = small_sb[:, U:U + SLOTS]
        first_wins = small_sb[:, U + SLOTS:]
        tok_sb = sb("tok_sb", [P, U])
        nowhere_row = sb("nowhere_row", [P, ROW])
        mhalf = sb("mhalf", [P, 1])
        warm = sb("warm", [P, 1])

        st = {k: sb(f"st_{k}", [P, 6]) for k in "psx"}
        mv = {k: sb(f"mv_{k}", [P, 2]) for k in "psx"}
        ve = {k: sb(f"ve_{k}", [P, 1]) for k in "psx"}
        rs = {k: sb(f"rs_{k}", [P, 1]) for k in "psx"}
        xn = {k: sb(f"xn_{k}", [P, D]) for k in "psx"}
        xnT = sb("xnT", [P, D])
        pn = sb("pn", [P, D])
        pT = sb("pT", [P, G, S])
        q_bd = {"s": [sb(f"q_bd_s{i}", [P, G, P]) for i in range(2)], "x": [sb("q_bd_x", [P, G, P])] * 2}
        k_hd = {k: [sb(f"k_hd_{k}{i}", [P, G, HG, S]) for i in range(2)] for k in "sx"}
        v_bd = {k: [sb(f"v_bd_{k}{i}", [P, VALL]) for i in range(2)] for k in "sx"}
        mx = {k: sb(f"mx_{k}", [P, G, HG]) for k in "sx"}
        pr = {k: sb(f"pr_{k}", [P, G, HG, S]) for k in "sx"}
        prT = {k: sb(f"prT_{k}", [P, G, 4, P]) for k in "sx"}
        rden = {k: sb(f"rden_{k}", [P, HP, 2]) for k in "sx"}
        on = {k: sb(f"on_{k}", [P, HP, 2, DK]) for k in "sx"}
        orow = [sb(f"orow{i}", [P, D]) for i in range(2)]
        onT = sb("onT", [P, D])
        hT = sb("hT", [P, D])

        bank = [ctx.enter_context(nc.psum_tensor(f"bank{i}", [P, 512], F32)) for i in range(8)]
        ps_s = {"s": [bank[0], bank[1]], "x": [bank[2], bank[3]]}
        ps_o = {"s": bank[4], "x": bank[5]}
        ps_xT = ps_p = ps_pT = bank[6][:, 0:P]
        ps_r = bank[6][:, 512 - U * E:].rearrange("p (u e) -> p u e", e=E)
        ps_qT = ps_oT = ps_wo = ps_hT = bank[7][:, 0:P]

        rowb = [sb(f"rowb{i}", [P, ROW]) for i in range(NROW)]
        place = [sb(f"place{i}", [P, 1], I32) for i in range(NROW)]
        token = [sb(f"token{i}", [P, 1], I32) for i in range(NROW)]
        yrow = [sb(f"yrow{i}", [P, D]) for i in range(NROW)]
        fx = [sb(f"fx{i}", [P, D]) for i in range(2)]
        fhT = [sb(f"fhT{i}", [P, D]) for i in range(2)]
        wtile = [sb(f"wtile{i}", [P, 2 * I]) for i in range(2)]
        gT = [sb(f"gT{i}", [P, CH, P]) for i in range(2)]
        ps_gate = [bank[0], bank[1]]
        ps_up = [bank[2], bank[3]]
        ps_y = [bank[6][:, 0:D], bank[7][:, 0:D]]
        ps_fhT = [bank[4][:, 0:P], bank[5][:, 0:P]]
        rt = {n: sb(f"rt_{n}", [P, U, E]) for n in ("l", "cl", "q", "pr", "t", "ml", "key", "eq", "oh")}
        r1 = {n: sb(f"r1_{n}", [P, U]) for n in ("max", "win", "q", "p", "tw", "rtw", "c1", "pos")}
        meta = sb("meta", [P, U, 2])
        et = {n: sb(f"et_{n}", [P, E, U]) for n in ("pad", "incl", "pos", "cmp")}
        e1 = {n: sb(f"e1_{n}", [P, E]) for n in ("n", "tiles", "ctiles")}
        se_cmp = sb("se_cmp", [P, SLOTS, E])
        se_f = sb("se_f", [P, SLOTS])
        slot_expert = sb("slot_expert", [P, SLOTS], I32)
        ps_pre, ps_tot = bank[4][:, 0:E * U], bank[4][:, E * U:2 * E * U]

        load = lambda eng, dst, src, name: eng.dma_start(dst, src).then_inc(sem(name), 16)

        def at(unit):
            return unit + 1

        def steps(eng, body, n, head, tail, turn=2):
            for t in range(head):
                body(t, t % turn)
            with eng.Fori(0, (n - head - tail) // turn) as i:
                for k in range(turn):
                    body(i * turn + (head + k), (head + k) % turn)
            for t in range(n - tail, n):
                body(t, t % turn)

        DELAY = {"n": 0, "p": 1, "s": 2, "o": 3, "w": 4, "x": 5, "y": 6, "r": 7}
        A_STEPS, A_PEEL, A_LOOP_END = U + 7, 8, U

        def phase_a(eng, body):
            def one(pair, par, fixed):
                u = {k: pair * 2 + (par - d) for k, d in DELAY.items()}
                parity = {k: (par - d) % 2 for k, d in DELAY.items()}
                u.update({f"{k} pair": pair + (par - d) // 2 for k, d in DELAY.items()})
                body(u, parity, lambda k: not fixed or 0 <= u[k] < U)

            for t in range(A_PEEL):
                one(t // 2, t % 2, True)
            with eng.Fori(A_PEEL // 2, A_LOOP_END // 2) as pair:
                for par in range(2):
                    one(pair, par, False)
            for t in range(A_LOOP_END, A_STEPS):
                one(t // 2, t % 2, True)

        def wait_apart(eng, *waits):
            waits = [(name, value if isinstance(value, int) else eng.snap(eng.to_reg(value))) for name, value in waits]
            eng.wait_ge(sem("ready"), 1)
            for name, value in waits:
                eng.wait_ge(sem(name), value)

        def expert_of(s, engine):
            return nc.values_load_multi_w_load_instructions(
                slot_expert[0:1, s:s + 1] if isinstance(s, int) else slot_expert[0:1, bass.ds(s, 1)],
                engines=[engine], min_val=0, max_val=E - 1,
                skip_runtime_bounds_check_because="a count of 0/1 comparisons, clamped to E - 1 by DVE")[1][0]

        def early_unit(u):
            return isinstance(u, int) and u < 2

        def first_unit(u):
            return isinstance(u, int) and u < 1

        block = ctx.enter_context(nc.Block())

        o_dram = nc.dram_tensor("attention_out", (U, NB, H, S, DK), F32, kind="Internal").ap()
        o_rows = o_dram.rearrange("u b h q d -> (u b h q d)").rearrange("(u p c) -> u p c", p=P, c=D)
        hs_dram = nc.dram_tensor("sorted_rows", (SLOTS * P, ROW), F32, kind="Internal").ap()
        hs_tiles = hs_dram.rearrange("(s p) c -> p s c", p=P)

        @block.sync
        def _(sp):
            xv = x.rearrange("(u p) d -> p u d", p=P)
            load(sp, x_all[:, 0:2, :], xv[:, 0:2, :], "l_x0")
            load(sp, id_sb[:], ident, "l_first")
            load(sp, wv_sb[:], wv, "l_first")
            load(sp, bv_sb[:], bv.partition_broadcast(P), "l_first")
            load(sp, hmask_sb[:], hmask, "l_first")
            load(sp, bo_sb[:], bo.partition_broadcast(P), "l_first")
            load(sp, x_all[:, 2:8, :], xv[:, 2:8, :], "l_x1")
            load(sp, wo_sb[:], wo, "l_second")
            load(sp, rw_sb[:], rw, "l_second")
            load(sp, x_all[:, 8:U, :], xv[:, 8:U, :], "l_x2")

            def body(u, par, live):
                if isinstance(u["n"], int) and u["n"] < 2:
                    load(sp, [ck_all, cv_all][u["n"]][:], [ctxk, ctxv][u["n"]], "l_ctx")
                if isinstance(u["n"], int) and u["n"] == 2:
                    load(sp, rb_sb[:], rb.partition_broadcast(P), "l_router")
                    load(sp, small_sb[:], small.partition_broadcast(P), "l_router")
                    load(sp, tok_sb[:], tokens, "l_router")
                    load(sp, tri_sb[:], tri, "l_router")
                if isinstance(u["n"], int) and 4 <= u["n"] < 8:
                    c = u["n"] - 4
                    if c == CH:
                        load(sp, wup_sb[:], wup, "l_w")
                    elif c < CH - 1:
                        load(sp, wdn_sb[:, :, c, :], wdn[:, c * P:(c + 1) * P, :].rearrange("e i c -> i e c"), "l_w")
                    else:
                        load(sp, wdn_sb[P - LAST:P, :, c, :], wdn[:, c * P:I, :].rearrange("e i c -> i e c"), "l_w")
                if live("s"):
                    sp.wait_ge(sem("s_on"), at(u["s"]))
                    for b in range(NB):
                        load(sp, o_dram[u["s"], b, :, :, :].rearrange("h q d -> q h d"),
                             on["s"][S * b:S * (b + 1), :, :, :].rearrange("p a c d -> p (a c) d"), "s_out")
                    wait_apart(sp, ("s_out", 16 * NB * at(u["s"])),
                               *([] if early_unit(u["s"]) else [("s_oT", at(u["s"]) - 2)]))
                    load(sp, orow[par["s"]][:], o_rows[u["s"], :, :], f"w_rows{par['s']}")

                if live("s"):
                    load(sp, hs_tiles[:, u["s"], :], nowhere_row[:, :], "prefilled")

            sp.wait_ge(sem("nowhere"), 1)
            load(sp, hs_tiles[:, U:SLOTS, :],
                 nowhere_row[:, :].unsqueeze(1).broadcast_to([P, SLOTS - U, ROW]), "prefilled")
            phase_a(sp, body)

            for n in range(NROW):
                sp.wait_ge(sem(f"b_sent{n}"), 16 * (U // NROW))
            load(sp, hs_all[:, 0, :], hs_tiles[:, 0, :], "c_row0")
            load(sp, hs_all[:, 1, :], hs_tiles[:, 1, :], "c_row1")
            with sp.Fori(0, (SLOTS - 2) // 2) as i:
                for k in range(2):
                    sp.wait_ge(sem(f"c_row{k}"), i * 16 + 16)
                    load(sp, hs_all[:, i * 2 + (2 + k), :], hs_tiles[:, i * 2 + (2 + k), :], f"c_row{k}")

        N_FIRST, N_SECOND, N_ROUTER = 16 * 5, 16 * 2, 16 * 4

        ones_in_v = lambda v, h2: v[S * h2:S * (h2 + 1), 0:HP * VW].rearrange(
            "p (a b c d) -> p a b c d", a=HP, b=NB, c=2)[:, :, :, h2, DK:DK + 1]

        def v_slots(v, h2):
            return v[S * h2:S * (h2 + 1), 0:HP * VW].rearrange(
                "p (a b c d) -> p a b c d", a=HP, b=NB, c=2)[:, :, :, h2, 0:DK]

        @block.gpsimd
        def _(pool):
            nc.gpsimd.memset(nowhere_row[:, 0:TOK], 0.0)
            nc.gpsimd.memset(nowhere_row[:, TOK:ROW], NOWHERE).then_inc(sem("nowhere"), 1)
            nc.gpsimd.memset(mhalf[:], -0.5).then_inc(sem("ready"), 1)
            for i in range(2):
                nc.gpsimd.memset(q_bd["s"][i][:], 0.0)
            nc.gpsimd.memset(q_bd["x"][0][:], 0.0).then_inc(sem("zeros"), 1)
            nc.gpsimd.memset(et["pad"][:], 0.0).then_inc(sem("pad_zero"), 1)
            nc.gpsimd.memset(wdn_sb[0:P - LAST, :, CH - 1, :], 0.0).then_inc(sem("overlap_zero"), 1)
            for k in "sx":
                for i in range(2):
                    nc.gpsimd.memset(v_bd[k][i][:], 0.0).then_inc(sem("v_zero"), 1)
            pool.wait_ge(sem("v_zero"), 4)
            for k in "sx":
                for i in range(2):
                    for h2 in range(2):
                        nc.gpsimd.memset(ones_in_v(v_bd[k][i], h2), 1.0).then_inc(sem("v_ones"), 1)
            pool.wait_ge(sem("v_ones"), 8)
            pool.wait_ge(sem("ready"), 1)

            def rstd(k, u):
                pool.wait_ge(sem(f"{k}_ve"), at(u))
                nc.gpsimd.tensor_tensor(rs[k][:], ve[k][:], mhalf[:], ALU.pow).then_inc(sem(f"{k}_rs"), 1)

            def by_head(k, par, src, u):
                if not early_unit(u):
                    pool.wait_ge(sem(f"{k}_sc"), at(u) * 2 - 4)
                nc.gpsimd.tensor_tensor(
                    k_hd[k][par][:], src.unsqueeze(2).broadcast_to([P, G, HG, S]),
                    hmask_sb[:, 0:HG].unsqueeze(1).unsqueeze(3).broadcast_to([P, G, HG, S]),
                    ALU.mult).then_inc(sem(f"{k}_khd"), 1)

            def body(u, par, live):
                if live("r"):
                    rstd("x", u["r"])
                if live("x"):
                    if first_unit(u["x"]):
                        pool.wait_ge(sem("l_ctx"), 32)
                    by_head("x", par["x"], ck_all[:, u["x"], :].rearrange("p (g k) -> p g k", g=G), u["x"])
                    if not early_unit(u["x"]):
                        wait_apart(pool, ("x_pv", at(u["x"]) * 2 - 4))
                    nc.gpsimd.tensor_tensor(
                        v_bd["x"][par["x"]][:, 0:HP * VW].rearrange("p (a c d) -> p a c d", c=2, d=DK + 1)[:, :, :, 0:DK],
                        cv_all[:, u["x"], :].rearrange("p (a d) -> p a d", d=DK).unsqueeze(2).broadcast_to([P, HP * NB, 2, DK]),
                        hmask_sb[:, HG:HG + 2].unsqueeze(1).unsqueeze(3).broadcast_to([P, HP * NB, 2, DK]),
                        ALU.mult).then_inc(sem("x_v"), 1)
                if live("n"):
                    rstd("p", u["n"])
                if live("w"):
                    rstd("s", u["w"])
                if live("p"):
                    if first_unit(u["p"]):
                        pool.wait_ge(sem("l_first"), N_FIRST)
                    pool.wait_ge(sem("p_xn"), at(u["p"]))
                    nc.gpsimd.tensor_tensor(x_all[:, u["p"], :], x_all[:, u["p"], :], bo_sb[:], ALU.add).then_inc(sem("p_xb"), 1)
                    pool.wait_ge(sem("p_pT"), at(u["p"]))
                    by_head("s", par["p"], pT[:, :, :], u["p"])
                if live("r"):
                    wait_apart(pool, ("x_xn", at(u["r"])))
                    nc.gpsimd.tensor_copy(h_all[:, u["r"], :], xn["x"][:]).then_inc(sem("x_h"), 1)

            phase_a(pool, body)

            pool.wait_ge(sem("prefilled"), 16 * (U + 1))

            def send(n, p):
                wait_apart(pool, ("f_y", at(n)))
                pool.indirect_dma_start(
                    out=hs_dram, out_offset=bass.IndirectOffsetOnAxis(ap=place[p][:, 0:1], axis=0),
                    in_=rowb[p][:, :], in_offset=None).then_inc(sem(f"b_sent{p}"), 16)

            steps(pool, send, U, 0, 0, turn=NROW)

            def put(s, p):
                wait_apart(pool, ("f_y", at(s + U)))
                pool.indirect_dma_start(
                    out=out, out_offset=bass.IndirectOffsetOnAxis(ap=token[p][:, 0:1], axis=0),
                    in_=yrow[p][:, :], in_offset=None,
                    bounds_check=NTOK - 1, oob_is_err=False).then_inc(sem(f"c_put{p}"), 16)

            steps(pool, put, SLOTS, 0, SLOTS % NROW, turn=NROW)
            for q in range(NROW):
                pool.wait_ge(sem(f"c_put{q}"), 16 * len(range(q, SLOTS, NROW)))

        @block.tensor
        def _(pe):
            pe.wait_ge(sem("l_first"), N_FIRST)
            pe.wait_ge(sem("zeros"), 1)
            pe.wait_ge(sem("v_ones"), 8)

            def scores(k, par, u, g):
                if g == 0:
                    pe.wait_ge(sem(f"{k}_khd"), at(u))
                    pe.wait_ge(sem(f"{k}_qbd"), at(u))
                if not first_unit(u):
                    pe.wait_ge(sem(f"{k}_prT{g}"), at(u) - 1)
                nc.tensor.matmul(ps_s[k][g][:, :], q_bd[k][par][:, g, :],
                                 k_hd[k][par][:, g, :, :].rearrange("p h k -> p (h k)"),
                                 start=True, stop=True).then_inc(sem(f"{k}_sc"), 1)

            def turn(k, u, g):
                pe.wait_ge(sem(f"{k}_exp{g}"), at(u))
                for i in range(4):
                    last = nc.tensor.transpose(ps_s[k][g][:, i * P:(i + 1) * P],
                                               pr[k][:, g, 2 * i:2 * i + 2, :].rearrange("p h k -> p (h k)"), id_sb[:])
                last.then_inc(sem(f"{k}_turn{g}"), 1)

            def weigh(k, par, u, g):
                pe.wait_ge(sem(f"{k}_prT{g}"), at(u))
                if g == 0:
                    pe.wait_ge(sem(f"{k}_v"), at(u))
                    if not first_unit(u):
                        pe.wait_ge(sem(f"{k}_on"), at(u) - 1)
                for i in range(4):
                    at_col = (4 * g + i) * VW
                    last = nc.tensor.matmul(ps_o[k][:, at_col:at_col + P], prT[k][:, g, i, :],
                                            v_bd[k][par][:, at_col:at_col + P], start=True, stop=True)
                last.then_inc(sem(f"{k}_pv"), 1)

            def reached(u, ahead):
                return min(at(u) + ahead, U) if isinstance(u, int) else at(u) + ahead

            def body(u, par, live):
                if live("p"):
                    pe.wait_ge(sem("p_xn"), at(u["p"]))
                    if not first_unit(u["p"]):
                        pe.wait_ge(sem("s_qbd"), at(u["p"]) - 1)
                    nc.tensor.transpose(ps_xT, xn["p"][:], id_sb[:]).then_inc(sem("p_xT"), 1)
                if live("x"):
                    pe.wait_ge(sem("s_xn"), at(u["x"]))
                    if not (isinstance(u["x"], int) and u["x"] < 3):
                        pe.wait_ge(sem("r_hTall"), at(u["x"]) - 3)
                    nc.tensor.transpose(ps_qT, xn["s"][:], id_sb[:]).then_inc(sem("s_qT"), 1)
                if live("s"):
                    scores("s", par["s"], u["s"], 0)
                if live("y"):
                    turn("x", u["y"], 0)
                if live("w"):
                    if first_unit(u["w"]):
                        pe.wait_ge(sem("l_second"), N_SECOND)
                    pe.wait_ge(sem(f"w_rows{par['w']}"), at(u["w pair"]) * 16)
                    if not first_unit(u["w"]):
                        pe.wait_ge(sem("x_qbd"), at(u["w"]) - 1)
                    nc.tensor.transpose(ps_oT, orow[par["w"]][:], id_sb[:]).then_inc(sem("s_oT"), 1)
                if live("s"):
                    scores("s", par["s"], u["s"], 1)
                if live("y"):
                    turn("x", u["y"], 1)
                if live("p"):
                    pe.wait_ge(sem("p_xnT"), at(u["p"]))
                    nc.tensor.matmul(ps_p, xnT[:], wv_sb[:], start=True, stop=True).then_inc(sem("p_p"), 1)
                if live("w"):
                    pe.wait_ge(sem("s_onT"), at(u["w"]))
                    nc.tensor.matmul(ps_wo, onT[:], wo_sb[:], start=True, stop=True).then_inc(sem("s_wo"), 1)
                if live("y"):
                    weigh("x", par["y"], u["y"], 0)
                    weigh("x", par["y"], u["y"], 1)
                if live("x"):
                    scores("x", par["x"], u["x"], 0)
                if live("s"):
                    turn("s", u["s"], 0)
                if live("p"):
                    pe.wait_ge(sem("p_pn"), at(u["p"]))
                    nc.tensor.transpose(ps_pT, pn[:], id_sb[:]).then_inc(sem("p_T"), 1)
                if live("x"):
                    scores("x", par["x"], u["x"], 1)
                if live("s"):
                    turn("s", u["s"], 1)
                if live("r"):
                    pe.wait_ge(sem("x_xn"), at(u["r"]))
                    pe.wait_ge(sem("s_x"), reached(u["r"], 3))
                    pe.wait_ge(sem("x_qbd"), reached(u["r"], 2))
                    if not live("x"):
                        pe.wait_ge(sem("r_hTall"), at(u["r"]) - 1)
                    nc.tensor.transpose(ps_hT, xn["x"][:], id_sb[:]).then_inc(sem("r_hT"), 1)
                if live("s"):
                    weigh("s", par["s"], u["s"], 0)
                    weigh("s", par["s"], u["s"], 1)
                if live("r"):
                    pe.wait_ge(sem("r_hTs"), at(u["r"]))
                    pe.wait_ge(sem("s_qbd"), reached(u["r"], 6))
                    nc.tensor.matmul(ps_r[:, u["r"], :], hT[:], rw_sb[:], start=True, stop=True).then_inc(sem("r_r"), 1)

            phase_a(pe, body)

            pe.wait_ge(sem("l_w"), 16 * (1 + CH))
            pe.wait_ge(sem("overlap_zero"), 1)
            pe.wait_ge(sem("r_hTall"), U)

            def up(n, p, weights, tokens):
                for ps, first, done in ((ps_gate, 0, "f_gate"), (ps_up, I, "f_up")):
                    for c in range(CH):
                        start = first + min(c * P, I - P)
                        last = nc.tensor.matmul(ps[p][:, c * P:(c + 1) * P], weights[:, start:start + P], tokens,
                                                start=True, stop=True)
                    last.then_inc(sem(done), 1)

            def down(n, p, expert):
                pe.wait_ge(sem("f_g"), at(n))
                if not early_unit(n):
                    pe.wait_ge(sem("f_y"), at(n) - 2)
                for c in range(CH):
                    last = nc.tensor.matmul(ps_y[p], gT[p][:, c, :], wdn_sb[:, expert, c, :], start=(c == 0), stop=(c == CH - 1))
                last.then_inc(sem("f_down"), 1)

            def shared_up(n, p):
                up(n, p, wup_sb[:, E, :], hT_all[:, n, :])

            def shared(n, p):
                down(n, p, E)
                if not (isinstance(n, int) and n + 2 >= U):
                    shared_up(n + 2, p)

            shared_up(0, 0)
            shared_up(1, 1)
            pe.wait_ge(sem("l_router"), N_ROUTER)
            pe.wait_ge(sem("chosen"), 1)
            by_et = rt["oh"][:].rearrange("p u e -> p e u")
            nc.tensor.matmul(ps_pre, tri_sb[:, 0, :], by_et, start=True, stop=True)
            nc.tensor.matmul(ps_tot, tri_sb[:, 1, :], by_et, start=True, stop=True).then_inc(sem("counted"), 1)
            steps(pe, shared, U, 4, 2)

            def to_hT(s, p):
                pe.wait_ge(sem("c_fx"), at(s))
                if not early_unit(s):
                    pe.wait_ge(sem("f_hT"), at(s) - 2)
                nc.tensor.transpose(ps_fhT[p], fx[p][:], id_sb[:]).then_inc(sem("c_hT"), 1)

            def routed_up(s, p):
                pe.wait_ge(sem("c_w"), at(s))
                pe.wait_ge(sem("f_hT"), at(s))
                up(s + U, p, wtile[p][:], fhT[p][:])

            def routed(s, p):
                tail = isinstance(s, int)
                down(s + U, p, expert_of(s, mybir.EngineType.PE))
                if not (tail and s + 3 >= SLOTS):
                    to_hT(s + 3, 1 - p)
                if not (tail and s + 2 >= SLOTS):
                    routed_up(s + 2, p)

            pe.wait_ge(sem("experts"), 1)
            to_hT(0, 0)
            to_hT(1, 1)
            routed_up(0, 0)
            to_hT(2, 0)
            routed_up(1, 1)
            steps(pe, routed, SLOTS, 2, 4)

        @block.scalar
        def _(act):
            act.wait_ge(sem("ready"), 1)
            nc.scalar.activation(warm[:], mhalf[:], ACT.Exp)
            act.wait_ge(sem("zeros"), 1)

            def block_diagonal(k, par, u, src, wait):
                act.wait_ge(sem(wait), at(u))
                if k == "s":
                    if not early_unit(u):
                        act.wait_ge(sem("s_sc"), at(u) * 2 - 4)
                elif not first_unit(u):
                    act.wait_ge(sem("x_sc"), at(u) * 2 - 2)
                for g in range(G):
                    for b in range(NB):
                        last = nc.scalar.copy(q_bd[k][par][S * b:S * (b + 1), g, S * b:S * (b + 1)],
                                              src[S * g:S * (g + 1), S * b:S * (b + 1)])
                last.then_inc(sem(f"{k}_qbd"), 1)

            def exp(k, u, g):
                act.wait_ge(sem(f"{k}_sub{g}"), at(u))
                nc.scalar.activation(pr[k][:, g, :, :], pr[k][:, g, :, :], ACT.Exp,
                                     scale=float(DK) ** -0.5).then_inc(sem(f"{k}_exp{g}"), 1)

            def turned(k, u, g):
                act.wait_ge(sem(f"{k}_turn{g}"), at(u))
                if not first_unit(u):
                    act.wait_ge(sem(f"{k}_pv"), 2 * at(u) - 3 + g)
                nc.scalar.copy(prT[k][:, g, :, :].rearrange("p i q -> p (i q)"), ps_s[k][g][:, :]).then_inc(sem(f"{k}_prT{g}"), 1)

            def body(u, par, live):
                if live("p"):
                    act.wait_ge(sem("p_xT"), at(u["p"]))
                    nc.scalar.copy(xnT[:], ps_xT).then_inc(sem("p_xnT"), 1)
                if live("x"):
                    block_diagonal("x", par["x"], u["x"], ps_qT, "s_qT")
                if live("w"):
                    act.wait_ge(sem("s_oT"), at(u["w"]))
                    nc.scalar.copy(onT[:], ps_oT).then_inc(sem("s_onT"), 1)
                if live("y"):
                    turned("x", u["y"], 0)
                    turned("x", u["y"], 1)
                if live("s"):
                    exp("s", u["s"], 0)
                    exp("s", u["s"], 1)
                if live("p"):
                    act.wait_ge(sem("p_pn"), at(u["p"]))
                    if not early_unit(u["p"]):
                        act.wait_ge(sem("s_pv"), at(u["p"]) * 2 - 4)
                    for b in range(NB):
                        for h2 in range(2):
                            src = pn[S * b:S * (b + 1), :].rearrange("p (a c d) -> p a c d", a=HP, c=2)[:, :, h2, :]
                            last = nc.scalar.copy(v_slots(v_bd["s"][par["p"]], h2)[:, :, b, :], src)
                    last.then_inc(sem("s_v"), 1)
                    act.wait_ge(sem("p_T"), at(u["p"]))
                    if not first_unit(u["p"]):
                        act.wait_ge(sem("s_khd"), at(u["p"]) - 1)
                    for g in range(G):
                        for b in range(NB):
                            last = nc.scalar.copy(pT[S * b:S * (b + 1), g, :], ps_pT[S * g:S * (g + 1), S * b:S * (b + 1)])
                    last.then_inc(sem("p_pT"), 1)
                if live("s"):
                    turned("s", u["s"], 0)
                if live("p"):
                    block_diagonal("s", par["p"], u["p"], ps_pT, "p_T")
                if live("s"):
                    turned("s", u["s"], 1)
                if live("r"):
                    act.wait_ge(sem("r_hT"), at(u["r"]))
                    if not first_unit(u["r"]):
                        act.wait_ge(sem("r_r"), at(u["r"]) - 1)
                    nc.scalar.copy(hT[:], ps_hT).then_inc(sem("r_hTs"), 1)
                    nc.scalar.copy(hT_all[:, u["r"], :], ps_hT).then_inc(sem("r_hTall"), 1)
                if live("x"):
                    exp("x", u["x"], 0)
                    exp("x", u["x"], 1)

            phase_a(act, body)

            def silu(n, p):
                act.wait_ge(sem("f_gate"), at(n))
                if not early_unit(n):
                    act.wait_ge(sem("f_down"), at(n) - 2)
                nc.scalar.activation(gT[p][:].rearrange("p c q -> p (c q)"), ps_gate[p][:, 0:CH * P],
                                     ACT.Silu).then_inc(sem("f_act"), 1)

            act.wait_ge(sem("clipped"), 1)
            nc.scalar.activation(rt["q"][:], rt["cl"][:], ACT.Exp, scale=-1.0).then_inc(sem("exped"), 1)
            steps(act, silu, U, 2, 0)

            def tile_weights(s, p):
                act.wait_ge(sem("f_up"), at(s + U) - 2)
                nc.scalar.copy(wtile[p][:], wup_sb[:, expert_of(s, mybir.EngineType.Activation), :]).then_inc(sem("c_w"), 1)

            def routed_hT(s, p):
                act.wait_ge(sem("c_hT"), at(s))
                act.wait_ge(sem("f_up"), at(s + U) - 2)
                nc.scalar.copy(fhT[p][:], ps_fhT[p]).then_inc(sem("f_hT"), 1)

            def routed(s, p):
                if not (isinstance(s, int) and s + 1 >= SLOTS):
                    silu(s + (U + 1), 1 - p)
                if not (isinstance(s, int) and s + 3 >= SLOTS):
                    routed_hT(s + 3, 1 - p)
                    tile_weights(s + 3, 1 - p)

            act.wait_ge(sem("experts"), 1)
            tile_weights(0, 0)
            tile_weights(1, 1)
            routed_hT(0, 0)
            routed_hT(1, 1)
            silu(U, 0)
            routed_hT(2, 0)
            tile_weights(2, 0)
            steps(act, routed, SLOTS, 3, 3)

        @block.vector
        def _(dve):
            done = [0]

            def link(ins):
                done[0] += 1
                ins.then_inc(sem("chain"), 1)
                dve.wait_ge(sem("chain"), done[0])

            def moments(k, src, u):
                nc.vector.bn_stats(st[k][:], src).then_inc(sem(f"{k}_st"), 1)

            def mean_variance(k, u):
                wait_apart(dve, (f"{k}_st", at(u)))
                nc.vector.bn_aggr(mv[k][:], st[k][:]).then_inc(sem(f"{k}_mv"), 1)

            def variance_eps(k, u):
                dve.wait_ge(sem(f"{k}_mv"), at(u))
                nc.vector.tensor_scalar(ve[k][:], mv[k][:, 1:2], EPS, None, ALU.add).then_inc(sem(f"{k}_ve"), 1)

            def normed(k, src, u):
                dve.wait_ge(sem(f"{k}_rs"), at(u))
                nc.vector.tensor_scalar(xn[k][:], src, mv[k][:, 0:1], rs[k][:, 0:1], ALU.subtract, ALU.mult).then_inc(sem(f"{k}_xn"), 1)

            def scores_of(k, g):
                return ps_s[k][g][:, :].rearrange("p (h k) -> p h k", h=HG)

            def maximum(k, u, g):
                dve.wait_ge(sem(f"{k}_sc"), 2 * at(u) - 1 + g)
                nc.vector.tensor_reduce(mx[k][:, g, :], scores_of(k, g), AX.X, ALU.max).then_inc(sem(f"{k}_mx"), 1)

            def soften(k, u, g):
                dve.wait_ge(sem(f"{k}_mx"), 2 * at(u) - 1 + g)
                if not first_unit(u):
                    dve.wait_ge(sem(f"{k}_turn{g}"), at(u) - 1)
                nc.vector.tensor_tensor(pr[k][:, g, :, :], scores_of(k, g), mx[k][:, g, :].unsqueeze(2).broadcast_to([P, HG, S]),
                                        ALU.subtract).then_inc(sem(f"{k}_sub{g}"), 1)

            def sums(k, b):
                return ps_o[k][S * b:S * (b + 1), 0:HP * VW].rearrange("p (a b c d) -> p a b c d", a=HP, b=NB, c=2)[:, :, b, :, :]

            def invert(k, u):
                dve.wait_ge(sem(f"{k}_pv"), 2 * at(u))
                for b in range(NB):
                    last = nc.vector.reciprocal(rden[k][S * b:S * (b + 1), :, :], sums(k, b)[:, :, :, DK])
                last.then_inc(sem(f"{k}_rden"), 1)

            def normalise(k, u):
                dve.wait_ge(sem(f"{k}_rden"), at(u))
                if k == "s" and not first_unit(u):
                    dve.wait_ge(sem("s_out"), 16 * NB * (at(u) - 1))
                for b in range(NB):
                    rows = slice(S * b, S * (b + 1))
                    last = nc.vector.tensor_tensor(on[k][rows, :, :, :], sums(k, b)[:, :, :, 0:DK],
                                                   rden[k][rows, :, :].unsqueeze(3).broadcast_to([S, HP, 2, DK]), ALU.mult)
                last.then_inc(sem(f"{k}_on"), 1)

            def body(u, par, live):
                x_of = lambda k: x_all[:, u[k], :]
                if live("o"):
                    invert("s", u["o"])
                if live("r"):
                    if not first_unit(u["r"]):
                        dve.wait_ge(sem("r_hT"), at(u["r"]) - 1)
                        dve.wait_ge(sem("x_h"), at(u["r"]) - 1)
                    normed("x", x_all[:, u["r"], :], u["r"])
                if live("o"):
                    normalise("s", u["o"])
                if live("s"):
                    maximum("s", u["s"], 0)
                if live("n"):
                    if isinstance(u["n"], int) and u["n"] in X_LOADS:
                        dve.wait_ge(sem(X_LOADS[u["n"]]), 16)
                    moments("p", x_all[:, u["n"], :], u["n"])
                if live("s"):
                    soften("s", u["s"], 0)
                    maximum("s", u["s"], 1)
                if live("p"):
                    if first_unit(u["p"]):
                        dve.wait_ge(sem("l_first"), N_FIRST)
                    dve.wait_ge(sem("p_p"), at(u["p"]))
                    if not first_unit(u["p"]):
                        dve.wait_ge(sem("p_T"), at(u["p"]) - 1)
                        dve.wait_ge(sem("s_v"), at(u["p"]) - 1)
                    nc.vector.tensor_tensor(pn[:], ps_p, bv_sb[:], ALU.add).then_inc(sem("p_pn"), 1)
                if live("s"):
                    soften("s", u["s"], 1)
                if live("n"):
                    mean_variance("p", u["n"])
                if live("w"):
                    dve.wait_ge(sem("p_xb"), at(u["w"]))
                    dve.wait_ge(sem("s_wo"), at(u["w"]))
                    nc.vector.tensor_tensor(x_of("w"), ps_wo, x_of("w"), ALU.add).then_inc(sem("s_x"), 1)
                if live("n"):
                    variance_eps("p", u["n"])
                if live("w"):
                    wait_apart(dve, ("s_x", at(u["w"])))
                    moments("s", x_of("w"), u["w"])
                    mean_variance("s", u["w"])
                if live("y"):
                    invert("x", u["y"])
                if live("w"):
                    variance_eps("s", u["w"])
                if live("n"):
                    if not first_unit(u["n"]):
                        dve.wait_ge(sem("p_xT"), at(u["n"]) - 1)
                    normed("p", x_all[:, u["n"], :], u["n"])
                if live("y"):
                    normalise("x", u["y"])
                if live("x"):
                    maximum("x", u["x"], 0)
                if live("y"):
                    dve.wait_ge(sem("x_on"), at(u["y"]))
                    nc.vector.tensor_tensor(x_of("y"), x_of("y"), on["x"][:].rearrange("p a b d -> p (a b d)"), ALU.add).then_inc(sem("x_x"), 1)
                if live("w"):
                    if not first_unit(u["w"]):
                        dve.wait_ge(sem("s_qT"), at(u["w"]) - 1)
                    normed("s", x_of("w"), u["w"])
                if live("x"):
                    soften("x", u["x"], 0)
                if live("y"):
                    wait_apart(dve, ("x_x", at(u["y"])))
                    moments("x", x_of("y"), u["y"])
                if live("x"):
                    maximum("x", u["x"], 1)
                if live("y"):
                    mean_variance("x", u["y"])
                if live("x"):
                    soften("x", u["x"], 1)
                if live("y"):
                    variance_eps("x", u["y"])

            X_LOADS = {0: "l_x0", 2: "l_x1", A_PEEL - 1: "l_x2"}
            phase_a(dve, body)

            def gated(n, p):
                dve.wait_ge(sem("f_act"), at(n))
                dve.wait_ge(sem("f_up"), at(n))
                g = gT[p][:].rearrange("p c q -> p (c q)")
                nc.vector.tensor_tensor(g, g, ps_up[p][:, 0:CH * P], ALU.mult).then_inc(sem("f_g"), 1)

            def shared_row(n, p, q, sent):
                if sent is not None:
                    dve.wait_ge(sem(f"b_sent{q}"), sent)
                nc.vector.tensor_copy(rowb[q][:, 0:D], h_all[:, n, :])
                nc.vector.tensor_copy(rowb[q][:, WT:ROW], meta[:, n, :])
                nc.vector.tensor_copy(place[q][:], r1["pos"][:, n:n + 1] if isinstance(n, int) else r1["pos"][:, bass.ds(n, 1)])
                dve.wait_ge(sem("f_down"), at(n))
                nc.vector.scalar_tensor_tensor(
                    rowb[q][:, D:2 * D], ps_y[p], r1["c1"][:, n:n + 1] if isinstance(n, int) else r1["c1"][:, bass.ds(n, 1)],
                    x_all[:, n, :], ALU.mult, ALU.add).then_inc(sem("f_y"), 1)
                dve.wait_ge(sem("f_y"), at(n))

            def b_step(n, k, sent):
                if not (isinstance(n, int) and n + 1 >= U):
                    gated(n + 1, (k + 1) % 2)
                if not first_unit(n):
                    shared_row(n - 1, (k - 1) % 2, (k - 1) % NROW, sent)

            bce = lambda a: a.unsqueeze(2).broadcast_to([P, U, E])
            bcu = lambda a: a.unsqueeze(1).broadcast_to([P, U, E])
            dve.wait_ge(sem("r_r"), U)
            dve.wait_ge(sem("l_router"), N_ROUTER)
            link(nc.vector.tensor_tensor(rt["l"][:], ps_r, bcu(rb_sb[:, :]), ALU.add))
            nc.vector.tensor_scalar(rt["cl"][:], rt["l"][:], -50.0, 50.0, ALU.max, ALU.min).then_inc(sem("clipped"), 1)
            dve.wait_ge(sem("exped"), 1)
            link(nc.vector.tensor_scalar(rt["q"][:], rt["q"][:], 1.0, None, ALU.add))
            nc.vector.tensor_scalar(rt["ml"][:], rt["cl"][:], KNEE, None, ALU.min)
            link(nc.vector.tensor_scalar(rt["t"][:], rt["q"][:], Q_KNEE, Q_KNEE, ALU.min, ALU.subtract))
            link(nc.vector.scalar_tensor_tensor(rt["key"][:], rt["t"][:], -8.0, rt["ml"][:], ALU.mult, ALU.add))
            link(nc.vector.tensor_reduce(r1["max"][:], rt["key"][:], AX.X, ALU.max))
            link(nc.vector.tensor_tensor(rt["eq"][:], rt["key"][:], bce(r1["max"][:, :]), ALU.is_ge))
            link(nc.vector.tensor_tensor(rt["t"][:], rt["eq"][:], bcu(first_wins), ALU.mult))
            link(nc.vector.tensor_reduce(r1["win"][:], rt["t"][:], AX.X, ALU.max))
            nc.vector.tensor_tensor(rt["oh"][:], rt["t"][:], bce(r1["win"][:, :]), ALU.is_equal).then_inc(sem("chosen"), 1)
            dve.wait_ge(sem("chosen"), 1)
            gated(0, 0)
            b_step(0, 0, None)
            weights = [
                lambda: nc.vector.tensor_tensor(rt["pr"][:], rt["q"][:], rt["oh"][:], ALU.mult),
                lambda: nc.vector.tensor_reduce(r1["q"][:], rt["pr"][:], AX.X, ALU.add),
                lambda: nc.vector.reciprocal(r1["p"][:], r1["q"][:]),
                lambda: nc.vector.tensor_scalar(r1["p"][:], r1["p"][:], 1e-8, 1.0 - 1e-8, ALU.max, ALU.min),
                lambda: nc.vector.tensor_scalar(r1["tw"][:], r1["p"][:], 0.5, 1e-8, ALU.add, ALU.add),
                lambda: nc.vector.tensor_scalar(r1["tw"][:], r1["tw"][:], 0.5, 2.0, ALU.max, ALU.min),
                lambda: nc.vector.reciprocal(r1["rtw"][:], r1["tw"][:]),
                lambda: nc.vector.tensor_scalar(r1["c1"][:], r1["rtw"][:], 0.5, None, ALU.mult),
                lambda: nc.vector.tensor_tensor(meta[:, :, 0], r1["rtw"][:], r1["p"][:], ALU.mult)]
            flat = lambda a: a.rearrange("p e u -> p (e u)")
            tot = ps_tot.rearrange("p (e u) -> p e u", e=E)
            places = [
                lambda: nc.vector.tensor_reduce(e1["n"][:], tot, AX.X, ALU.add),
                lambda: nc.vector.tensor_tensor(et["cmp"][:], e1["n"][:, :].unsqueeze(2).broadcast_to([P, E, U]),
                                                thr.unsqueeze(1).broadcast_to([P, E, U]), ALU.is_gt),
                lambda: nc.vector.tensor_reduce(e1["tiles"][:], et["cmp"][:], AX.X, ALU.add),
                lambda: nc.vector.scalar_tensor_tensor(et["pad"][:, 1:E, 0], e1["tiles"][:, 0:E - 1], float(P),
                                                       e1["n"][:, 0:E - 1], ALU.mult, ALU.subtract),
                lambda: nc.vector.tensor_tensor_scan(flat(et["incl"][:]), ps_tot, flat(et["pad"][:]), 0.0, ALU.add, ALU.add),
                lambda: nc.vector.tensor_tensor(flat(et["pos"][:]), flat(et["incl"][:]), ps_pre, ALU.add),
                lambda: nc.vector.tensor_tensor(et["pos"][:], et["pos"][:], rt["oh"][:].rearrange("p u e -> p e u"), ALU.mult),
                lambda: nc.vector.tensor_reduce(r1["pos"][:], et["pos"][:].rearrange("p e u -> p u e"), AX.X, ALU.add)]
            nc.vector.tensor_copy(meta[:, :, 1], tok_sb[:])
            dve.wait_ge(sem("counted"), 1)
            dve.wait_ge(sem("pad_zero"), 1)
            for k in range(max(len(weights), len(places))):
                for name, run in (("weight_steps", weights), ("place_steps", places)):
                    if k < len(run):
                        if k > 0:
                            dve.wait_ge(sem(name), k)
                        run[k]().then_inc(sem(name), 1)
            dve.wait_ge(sem("weight_steps"), len(weights))
            dve.wait_ge(sem("place_steps"), len(places))

            dve.wait_ge(sem("x_h"), U)
            PEEL = 6
            for n in range(1, PEEL):
                b_step(n, n, 16 * ((n - 1) // NROW) if n > NROW else None)
            link(nc.vector.tensor_tensor_scan(e1["ctiles"][:], e1["tiles"][:], et["pad"][:, 0, 0:E], 0.0, ALU.add, ALU.add))
            link(nc.vector.tensor_tensor(se_cmp[:], slot_no.unsqueeze(2).broadcast_to([P, SLOTS, E]),
                                         e1["ctiles"][:, :].unsqueeze(1).broadcast_to([P, SLOTS, E]), ALU.is_ge))
            link(nc.vector.tensor_reduce(se_f[:], se_cmp[:], AX.X, ALU.add))
            nc.vector.tensor_scalar(slot_expert[:], se_f[:], float(E - 1), None, ALU.min).then_inc(sem("experts"), 1)
            with dve.Fori(0, (U - PEEL - 2) // NROW) as i:
                for k in range(NROW):
                    b_step(i * NROW + (PEEL + k), PEEL + k, i * 16 + 16 * ((PEEL + k - 1) // NROW))
            for n in range(U - 2, U):
                b_step(n, n, 16 * ((n - 1) // NROW))
            shared_row(U - 1, (U - 1) % 2, (U - 1) % NROW, 16 * ((U - 1) // NROW))

            def routed_in(s, p, landed):
                dve.wait_ge(sem(f"c_row{p}"), landed)
                if not early_unit(s):
                    dve.wait_ge(sem("c_hT"), at(s) - 2)
                nc.vector.tensor_copy(fx[p][:], hs_all[:, s, 0:D]).then_inc(sem("c_fx"), 1)

            def routed_row(s, p, q, put):
                if put is not None:
                    dve.wait_ge(sem(f"c_put{q}"), put)
                nc.vector.tensor_copy(token[q][:], hs_all[:, s, TOK:ROW])
                dve.wait_ge(sem("f_down"), at(s + U))
                nc.vector.scalar_tensor_tensor(yrow[q][:], ps_y[p], hs_all[:, s, WT:WT + 1], hs_all[:, s, D:2 * D],
                                               ALU.mult, ALU.add).then_inc(sem("f_y"), 1)
                dve.wait_ge(sem("f_y"), at(s + U))

            def c_step(s, k, landed, put):
                if not (isinstance(s, int) and s + 1 >= SLOTS):
                    gated(s + (U + 1), (k + 1) % 2)
                if landed is not None:
                    routed_in(s + 4, k % 2, landed)
                if not first_unit(s):
                    routed_row(s - 1, (k - 1) % 2, (k - 1) % NROW, put)

            for s in range(3):
                routed_in(s, s % 2, 16 * (s // 2 + 1))
            gated(U, 0)
            routed_in(3, 1, 32)
            for s in range(PEEL):
                c_step(s, s, 16 * ((s + 4) // 2 + 1), 16 * ((s - 1) // NROW) if s > NROW else None)
            with dve.Fori(0, (SLOTS - 4 - PEEL) // NROW) as i:
                for k in range(NROW):
                    c_step(i * NROW + (PEEL + k), PEEL + k, i * (8 * NROW) + 16 * ((PEEL + k + 4) // 2 + 1),
                           i * 16 + 16 * ((PEEL + k - 1) // NROW))
            for s in range(SLOTS - 4, SLOTS):
                c_step(s, s, None, 16 * ((s - 1) // NROW))
            routed_row(SLOTS - 1, (SLOTS - 1) % 2, (SLOTS - 1) % NROW, 16 * ((SLOTS - 1) // NROW))


def kernel(**inputs):
    import numpy as np
    import concourse.bacc as bacc
    from concourse.bass_utils import run_bass_kernel_spmd

    a = {k: np.asarray(v) for k, v in inputs.items()}
    f32 = np.float32
    c = a["ctx_1024"]
    p = np.arange(P)
    arrays = {
        "x": a["x"].reshape(NTOK, D),
        "ctxk": c.reshape(U, NB, S, G, HG * DK).transpose(1, 4, 0, 3, 2).reshape(P, U, D),
        "ctxv": c.reshape(U, NB, S, HP, 2, DK).transpose(4, 2, 0, 3, 1, 5).reshape(P, U, D),
        "wv": a["L0_attn_Wv"].T, "bv": a["L0_attn_bv"], "wo": a["L0_attn_Wo"].T, "bo": a["L0_attn_bo"],
        "rw": a["L0_ffn_router_w"].T, "rb": a["L0_ffn_routing_bias"],
        "wup": np.concatenate([np.concatenate([a["L0_ffn_ew1"], a["L0_ffn_sw1"][None]]),
                               np.concatenate([a["L0_ffn_ew3"], a["L0_ffn_sw3"][None]])], axis=1).transpose(2, 0, 1),
        "wdn": np.concatenate([a["L0_ffn_ew2"], a["L0_ffn_sw2"][None]]).transpose(0, 2, 1),
        "ident": np.eye(P, dtype=f32),
        "hmask": np.concatenate([(p[:, None] // DK) % HG == np.arange(HG)[None],
                                 p[:, None] // S == np.arange(2)[None]], axis=1).astype(f32),
        "tri": np.stack([np.triu(np.ones((P, P), f32), 1) - 1, np.ones((P, P), f32)], axis=1),
        "small": np.concatenate([np.arange(U) * P, np.arange(SLOTS), E - np.arange(E)]).astype(f32),
        "tokens": (p[:, None] + P * np.arange(U)[None]).astype(f32),
    }
    arrays = {f"in_{k}": np.ascontiguousarray(v) for k, v in arrays.items()}
    nc = bacc.Bacc("TRN2", target_bir_lowering=False, num_devices=1)
    aps = [nc.dram_tensor(k, v.shape, mybir.dt.from_np(v.dtype), kind="ExternalInput").ap() for k, v in arrays.items()]
    out = nc.dram_tensor("out", (NTOK, D), F32, kind="ExternalOutput").ap()
    build(nc, *aps, out)
    r = run_bass_kernel_spmd(nc, [arrays], core_ids=[0])
    return r.results[0]["out"].reshape(B, S, D)
```
